# Optimizing a Trainium2 kernel written in Bass

```python
import numpy as np
import jax
import jax.numpy as jnp

def _softmax(x, axis=-1):
    return jax.nn.softmax(x, axis=axis)

def _gelu(x):
    return jax.nn.gelu(x, approximate=True)

def _silu(x):
    return jax.nn.silu(x)

def _sigmoid(x):
    return jax.nn.sigmoid(x)

def _layernorm(x, axis=-1, eps=1e-05):
    m = jnp.mean(x, axis=axis, keepdims=True)
    v = jnp.var(x, axis=axis, keepdims=True)
    return (x - m) / jnp.sqrt(v + eps)

def _scatter_add(tgt, idx, src, axis=0):
    return tgt.at[idx].add(src)

def _segment_sum(src, seg, n):
    return jax.ops.segment_sum(src, seg, n)
kernel_name = 'mk_xattn_ffn_d1_seqx_r4_7105f7'

def setup_inputs(seed: int=0):
    np.random.seed(seed)
    _w = jnp.asarray

    def _rec_inputs():
        import jax
        import jax.numpy as jnp
        _rk = jax.random.key(seed)
        x = -0.0002928 + 1 * jax.random.normal(jax.random.fold_in(_rk, 1), (8, 512, 256), jnp.float32)
        _lenS = 512 - jax.random.randint(jax.random.fold_in(_rk, 7), (8,), 0, max(1, 512 // 4) + 1, jnp.int32)
        _lenS2 = 64 - jax.random.randint(jax.random.fold_in(_rk, 8), (8,), 0, max(1, 64 // 4) + 1, jnp.int32)
        _ctx_1024P = jax.random.normal(jax.random.fold_in(_rk, 11), (8, 16, 256), jnp.float32)
        _ctx_1024c = jax.random.dirichlet(jax.random.fold_in(_rk, 511), 0.3 * jnp.ones((16,), jnp.float32), (8, 64))
        _ctx_1024t = jnp.einsum('bsk,bkd->bsd', _ctx_1024c, _ctx_1024P)
        _ctx_1024t = _ctx_1024t * jax.lax.rsqrt(jnp.mean(jnp.square(_ctx_1024t)) + 1e-12) * 0.953939
        ctx_1024 = -1.39393e-06 + 0.999914 * (_ctx_1024t + 0.3 * jax.random.normal(jax.random.fold_in(_rk, 611), (8, 64, 256), jnp.float32))
        return (x, ctx_1024)
    x, ctx_1024 = _rec_inputs()

    def _L0_xattn_setup():
        import jax, jax.numpy as jnp
        import numpy as np
        NUM_HEADS = 16
        D_MODEL = 256
        D_K = 64
        D_V = 64
        NEG_INF = -1000000000.0
        key = jax.random.key(seed)
        ks = jax.random.split(key, 7)
        B, S = (2, 512)
        Q = jax.random.normal(ks[0], (B, S, D_MODEL), dtype=jnp.float32)
        K = jax.random.normal(ks[1], (B, S, D_MODEL), dtype=jnp.float32)
        V = jax.random.normal(ks[2], (B, S, D_MODEL), dtype=jnp.float32)
        s = 1.0 / np.sqrt(D_MODEL)
        W_q = jax.random.normal(ks[3], (D_MODEL, D_K * NUM_HEADS), dtype=jnp.float32) * s
        W_k = jax.random.normal(ks[4], (D_MODEL, D_K), dtype=jnp.float32) * s
        W_v = jax.random.normal(ks[5], (D_MODEL, D_V), dtype=jnp.float32) * s
        W_o = jax.random.normal(ks[6], (D_V * NUM_HEADS, D_MODEL), dtype=jnp.float32) * (1.0 / np.sqrt(D_V * NUM_HEADS))
        return {'Q': Q, 'K': K, 'V': V, 'W_q': W_q, 'W_k': W_k, 'W_v': W_v, 'W_o': W_o}
    _L0_xattn_all = _L0_xattn_setup()
    _L0_xattn_in = {k: v for k, v in _L0_xattn_all.items() if k in ('W_q', 'W_k', 'W_v', 'W_o')}
    del _L0_xattn_all

    def _L0_ffn_setup():
        import jax, jax.numpy as jnp
        import numpy as np
        B, S, D = (8, 128, 256)
        H = 16
        DFF = 1024
        E = 4
        K = 2
        EPS = 1e-05

        def _layernorm(x, w, b):
            m = x.mean(-1, keepdims=True)
            v = ((x - m) ** 2).mean(-1, keepdims=True)
            return (x - m) / jnp.sqrt(v + EPS) * w + b

        def _encoder_layer(x, iw, ib, ow, ob, l1w, l1b, l2w, l2b, n1w, n1b, n2w, n2b):
            b, s, d = x.shape
            hd = d // H
            qkv = x @ iw.T + ib
            q, k, v = jnp.split(qkv, 3, axis=-1)
            rs = lambda t: t.reshape(b, s, H, hd).transpose(0, 2, 1, 3)
            q, k, v = (rs(q), rs(k), rs(v))
            scale = jnp.asarray(hd, x.dtype) ** 0.5
            scores = jnp.einsum('bhqd,bhkd->bhqk', q, k) / scale
            attn = jax.nn.softmax(scores, axis=-1)
            o = jnp.einsum('bhqk,bhkd->bhqd', attn, v).transpose(0, 2, 1, 3).reshape(b, s, d)
            o = o @ ow.T + ob
            x = _layernorm(x + o, n1w, n1b)
            ff = jax.nn.relu(x @ l1w.T + l1b) @ l2w.T + l2b
            return _layernorm(x + ff, n2w, n2b)
        key = jax.random.key(seed)
        ks = jax.random.split(key, 12)
        g = lambda k, shape: jax.random.normal(k, shape, dtype=jnp.float32) * 0.02
        return {'x': jax.random.normal(ks[0], (B, S, D), dtype=jnp.float32), 'in_proj_w': g(ks[1], (E, 3 * D, D)), 'in_proj_b': g(ks[2], (E, 3 * D)), 'out_proj_w': g(ks[3], (E, D, D)), 'out_proj_b': g(ks[4], (E, D)), 'ln1_w': jnp.ones((E, D), jnp.float32), 'ln1_b': jnp.zeros((E, D), jnp.float32), 'lin1_w': g(ks[5], (E, DFF, D)), 'lin1_b': g(ks[6], (E, DFF)), 'lin2_w': g(ks[7], (E, D, DFF)), 'lin2_b': g(ks[8], (E, D)), 'ln2_w': jnp.ones((E, D), jnp.float32), 'ln2_b': jnp.zeros((E, D), jnp.float32), 'gate_w': g(ks[9], (E, D)), 'gate_b': g(ks[10], (E,))}
    _L0_ffn_all = _L0_ffn_setup()
    _L0_ffn_in = {k: v for k, v in _L0_ffn_all.items() if k in ('in_proj_w', 'in_proj_b', 'out_proj_w', 'out_proj_b', 'ln1_w', 'ln1_b', 'lin1_w', 'lin1_b', 'lin2_w', 'lin2_b', 'ln2_w', 'ln2_b', 'gate_w', 'gate_b')}
    del _L0_ffn_all
    return {'x': x, 'ctx_1024': ctx_1024, 'L0_xattn_W_q': _L0_xattn_in['W_q'], 'L0_xattn_W_k': _L0_xattn_in['W_k'], 'L0_xattn_W_v': _L0_xattn_in['W_v'], 'L0_xattn_W_o': _L0_xattn_in['W_o'], 'L0_ffn_in_proj_w': _L0_ffn_in['in_proj_w'], 'L0_ffn_in_proj_b': _L0_ffn_in['in_proj_b'], 'L0_ffn_out_proj_w': _L0_ffn_in['out_proj_w'], 'L0_ffn_out_proj_b': _L0_ffn_in['out_proj_b'], 'L0_ffn_ln1_w': _L0_ffn_in['ln1_w'], 'L0_ffn_ln1_b': _L0_ffn_in['ln1_b'], 'L0_ffn_lin1_w': _L0_ffn_in['lin1_w'], 'L0_ffn_lin1_b': _L0_ffn_in['lin1_b'], 'L0_ffn_lin2_w': _L0_ffn_in['lin2_w'], 'L0_ffn_lin2_b': _L0_ffn_in['lin2_b'], 'L0_ffn_ln2_w': _L0_ffn_in['ln2_w'], 'L0_ffn_ln2_b': _L0_ffn_in['ln2_b'], 'L0_ffn_gate_w': _L0_ffn_in['gate_w'], 'L0_ffn_gate_b': _L0_ffn_in['gate_b']}

def reference(x, ctx_1024, L0_xattn_W_q, L0_xattn_W_k, L0_xattn_W_v, L0_xattn_W_o, L0_ffn_in_proj_w, L0_ffn_in_proj_b, L0_ffn_out_proj_w, L0_ffn_out_proj_b, L0_ffn_ln1_w, L0_ffn_ln1_b, L0_ffn_lin1_w, L0_ffn_lin1_b, L0_ffn_lin2_w, L0_ffn_lin2_b, L0_ffn_ln2_w, L0_ffn_ln2_b, L0_ffn_gate_w, L0_ffn_gate_b):
    import jax
    import jax.numpy as jnp

    def _L0_xattn_ref(Q, K, V, W_q, W_k, W_v, W_o):
        import jax, jax.numpy as jnp
        import numpy as np
        NUM_HEADS = 16
        D_MODEL = 256
        D_K = 64
        D_V = 64
        NEG_INF = -1000000000.0
        B, Sq, _ = Q.shape
        Sk = K.shape[1]
        q = (Q @ W_q).reshape(B, Sq, NUM_HEADS, D_K).transpose(0, 2, 1, 3)
        k = K @ W_k
        v = V @ W_v
        scores = jnp.einsum('bhqd,bkd->bhqk', q, k) / jnp.sqrt(jnp.float32(D_K))
        causal = jnp.tril(jnp.ones((Sq, Sk), dtype=bool))
        scores = jnp.where(causal[None, None], scores, NEG_INF)
        attn = jax.nn.softmax(scores, axis=-1)
        out = jnp.einsum('bhqk,bkd->bhqd', attn, v)
        out = out.transpose(0, 2, 1, 3).reshape(B, Sq, NUM_HEADS * D_V)
        return out @ W_o

    def _L0_ffn_ref(x, in_proj_w, in_proj_b, out_proj_w, out_proj_b, ln1_w, ln1_b, lin1_w, lin1_b, lin2_w, lin2_b, ln2_w, ln2_b, gate_w, gate_b):
        import jax, jax.numpy as jnp
        import numpy as np
        B, S, D = (8, 128, 256)
        H = 16
        DFF = 1024
        E = 4
        K = 2
        EPS = 1e-05

        def _layernorm(x, w, b):
            m = x.mean(-1, keepdims=True)
            v = ((x - m) ** 2).mean(-1, keepdims=True)
            return (x - m) / jnp.sqrt(v + EPS) * w + b

        def _encoder_layer(x, iw, ib, ow, ob, l1w, l1b, l2w, l2b, n1w, n1b, n2w, n2b):
            b, s, d = x.shape
            hd = d // H
            qkv = x @ iw.T + ib
            q, k, v = jnp.split(qkv, 3, axis=-1)
            rs = lambda t: t.reshape(b, s, H, hd).transpose(0, 2, 1, 3)
            q, k, v = (rs(q), rs(k), rs(v))
            scale = jnp.asarray(hd, x.dtype) ** 0.5
            scores = jnp.einsum('bhqd,bhkd->bhqk', q, k) / scale
            attn = jax.nn.softmax(scores, axis=-1)
            o = jnp.einsum('bhqk,bhkd->bhqd', attn, v).transpose(0, 2, 1, 3).reshape(b, s, d)
            o = o @ ow.T + ob
            x = _layernorm(x + o, n1w, n1b)
            ff = jax.nn.relu(x @ l1w.T + l1b) @ l2w.T + l2b
            return _layernorm(x + ff, n2w, n2b)
        gate_logits = x.mean(axis=1) @ gate_w.T + gate_b
        _, top_idx = jax.lax.top_k(gate_logits, K)
        gate_weights = jax.nn.softmax(gate_logits, axis=-1)
        mask = jnp.zeros_like(gate_weights).at[jnp.arange(x.shape[0])[:, None], top_idx].set(1.0)
        expert_outs = jax.vmap(_encoder_layer, in_axes=(None, 0, 0, 0, 0, 0, 0, 0, 0, 0, 0, 0, 0))(x, in_proj_w, in_proj_b, out_proj_w, out_proj_b, lin1_w, lin1_b, lin2_w, lin2_b, ln1_w, ln1_b, ln2_w, ln2_b)
        return jnp.einsum('be,ebsd->bsd', gate_weights * mask, expert_outs)
    x = x + _L0_xattn_ref(_layernorm(x, axis=-1), ctx_1024, ctx_1024, L0_xattn_W_q, L0_xattn_W_k, L0_xattn_W_v, L0_xattn_W_o)
    x = x + _L0_ffn_ref(_layernorm(x, axis=-1), L0_ffn_in_proj_w, L0_ffn_in_proj_b, L0_ffn_out_proj_w, L0_ffn_out_proj_b, L0_ffn_ln1_w, L0_ffn_ln1_b, L0_ffn_lin1_w, L0_ffn_lin1_b, L0_ffn_lin2_w, L0_ffn_lin2_b, L0_ffn_ln2_w, L0_ffn_ln2_b, L0_ffn_gate_w, L0_ffn_gate_b)
    return x

_drawn_inputs = setup_inputs


def setup_inputs(seed=0):
    import zlib

    import numpy as np

    out = dict(_drawn_inputs(seed))
    spreads = {'L0_ffn_ln1_w': (1.0, 0.2),
     'L0_ffn_ln1_b': (0.0, 0.355),
     'L0_ffn_ln2_w': (1.0, 0.2),
     'L0_ffn_ln2_b': (0.0, 0.346)}
    factors = {'L0_ffn_in_proj_w': 5.105,
     'L0_ffn_in_proj_b': 8.0,
     'L0_ffn_out_proj_w': 5.127,
     'L0_ffn_out_proj_b': 8.0,
     'L0_ffn_lin1_b': 28.209,
     'L0_ffn_lin2_b': 8.0,
     'L0_ffn_gate_b': 2.88}
    for name, (base, spread) in spreads.items():
        noise = np.random.default_rng([zlib.crc32(name.encode()), seed]).standard_normal(out[name].shape)
        drawn = base * np.exp(spread * noise) if base else spread * noise
        out[name] = jnp.asarray(drawn.astype(out[name].dtype))
    for name, factor in factors.items():
        out[name] = (out[name] * factor).astype(out[name].dtype)
    return out
```

```python
from contextlib import ExitStack

import concourse.bass as bass
from concourse import mybir

ALU = mybir.AluOpType
ACT = mybir.ActivationFunctionType
X = mybir.AxisListType.X
F32 = mybir.dt.float32
F32R = mybir.dt.float32r
I32 = mybir.dt.int32

P = 128
B, S, D = 8, 512, 256
T = S // P
C = D // P
SC = 64
H = 16
DK = 64
HD = D // H
E = 4
TOPK = 2
PAIRS = B * TOPK
F = 1024
M = F // P
EPS = 1e-5
NEG = -1e9
DMA = 16


def stage_a(nc, dram, x2_dram, x2T_dram, out, keep):
    with ExitStack() as ctx:
        def sb(name, shape, dt=F32):
            return ctx.enter_context(nc.sbuf_tensor(name, shape, dt))

        def sem(name):
            return ctx.enter_context(nc.semaphore(name))

        bank = [ctx.enter_context(nc.psum_tensor(f"a_bank{n}", [P, 512], F32)) for n in range(6, 8)]
        score_banks = [ctx.enter_context(nc.psum_tensor(f"a_scores{n}", [P, H * SC], F32)) for n in range(2)]
        attnT_bank = ctx.enter_context(nc.psum_tensor("a_attnT", [P, M, P], F32))
        turn_bank, out_bank = bank

        ident, colsum = keep["ident"], keep["colsum"]
        ctxT = sb("ctxT", [P, C, B * SC])
        Wk = sb("Wk", [P, C, DK])
        Wv = sb("Wv", [P, C, DK])
        WqT = sb("WqT", [DK, H, D])
        Wo = sb("Wo", [DK, H, D])
        kT = sb("kT", [DK, B * SC])
        vT = sb("vT", [DK, B, SC])
        vT_b = sb("vT_b", [DK, SC])
        G = sb("G", [P, C, H, B, SC])
        VW = sb("VW", [P, M, D])
        xt = sb("xt", [P, T, D])
        xn = sb("xn", [P, 2, D])
        xnT = sb("xnT", [P, 2, C, P])
        attn = sb("attn", [P, 2, H * SC])
        attnT = sb("attnT", [P, M, P])
        x1 = sb("x1", [P, T, D])
        x2 = sb("x2", [P, T, D])
        x2T = sb("x2T_a", [P, C, S])
        stats = sb("stats_a", [P, 6])
        mv = sb("mv_a", [P, 2])
        rstd = sb("rstd_a", [P, 1])
        spare = sb("spare_a", [P, 1])
        seen, hidden = sb("seen", [P, SC]), sb("hidden_a", [P, SC])
        var_eps = sb("var_eps_a", [P, 1])
        minus_half = sb("minus_half_a", [P, 1])
        mx = sb("mx", [P, H])
        total = sb("total", [P, H])
        rz = sb("rz", [P, 2, H])

        consts_in = sem("a_consts_in")
        x_in = [sem(f"a_x_in{t}") for t in range(T)]
        kv_mm, kv_sb = sem("a_kv_mm"), sem("a_kv_sb")
        g_mm, g_sb = sem("a_g_mm"), sem("a_g_sb")
        vTb_ready = sem("a_vTb_ready")
        vw_mm, vw_sb = sem("a_vw_mm"), sem("a_vw_sb")
        xn_ready, xnT_mm, xnT_sb = sem("a_xn_ready"), sem("a_xnT_mm"), sem("a_xnT_sb")
        scores_mm = sem("a_scores_mm")
        mask_set = sem("a_mask_set")
        shifted, exped = sem("a_shifted"), sem("a_exped")
        rz_ready, attn_ready = sem("a_rz_ready"), sem("a_attn_ready")
        attnT_mm, attnT_sb = sem("a_attnT_mm"), sem("a_attnT_sb")
        out_mm, x1_ready, x2_ready = sem("a_out_mm"), sem("a_x1_ready"), sem("a_x2_ready")
        x2T_mm, x2T_sb = sem("a_x2T_mm"), sem("a_x2T_sb")
        colsum_done = sem("a_colsum_done")
        tiles_stored, x2T_stored = sem("a_tiles_stored"), sem("a_x2T_stored")
        half_set, var_ready, rstd_ready = sem("a_half_set"), sem("a_var_ready"), sem("a_rstd_ready")
        dve_step = sem("a_dve_step")

        block = ctx.enter_context(nc.Block())

        @block.sync
        def _(sp):
            sp.sem_inc(tiles_stored, DMA)
            sp.sem_inc(x2T_stored, DMA)
            for dst, src in ((ctxT, dram["ctxT"].rearrange("(c p) n -> p c n", p=P)),
                             (Wk, dram["Wk"].rearrange("(c p) n -> p c n", p=P)),
                             (Wv, dram["Wv"].rearrange("(c p) n -> p c n", p=P)),
                             (WqT, dram["WqT"]), (Wo, dram["Wo"]), (ident, dram["ident"])):
                sp.dma_start(dst[:], src).then_inc(consts_in, DMA)
            for t in range(T):
                sp.dma_start(xt[:, t, :], dram["x"][0, t * P:(t + 1) * P, :]).then_inc(x_in[t], DMA)

            def finish_batch(b, prefetch):
                for t in range(T):
                    rows = slice(t * P, (t + 1) * P)
                    sp.wait_ge(x2_ready, b * T + (t + 1))
                    sp.dma_start(out[bass.ds(b, 1), rows, :].rearrange("o p d -> p (o d)"),
                                 x1[:, t, :]).then_inc(tiles_stored, DMA)
                    sp.dma_start(x2_dram[bass.ds(b, 1), rows, :].rearrange("o p d -> p (o d)"),
                                 x2[:, t, :]).then_inc(tiles_stored, DMA)
                    if prefetch:
                        sp.dma_start(xt[:, t, :], dram["x"][bass.ds(b + 1, 1), rows, :].rearrange(
                            "o p d -> p (o d)")).then_inc(x_in[t], DMA)
                sp.wait_ge(x2T_sb, b * T + T)
                sp.dma_start(x2T_dram[bass.ds(b, 1), :, :, :].rearrange("o p c n -> p (o c) n"),
                             x2T[:]).then_inc(x2T_stored, DMA)

            with sp.Fori(0, B - 1) as b:
                finish_batch(b, True)
            finish_batch(B - 1, False)
            sp.wait_ge(tiles_stored, B * T * 2 * DMA + DMA)
            sp.wait_ge(x2T_stored, B * DMA + DMA)

        @block.tensor
        def _(pe):
            pe.wait_ge(consts_in, 6 * DMA)
            for n, w in enumerate((Wk, Wv)):
                for c in range(C):
                    last = pe.matmul(bank[n][0:DK, :], w[:, c, :], ctxT[:, c, :], start=(c == 0), stop=(c == C - 1))
                last.then_inc(kv_mm, 1)
            pe.wait_ge(kv_sb, 2)
            for n in range(C * H):
                c, h = divmod(n, H)
                if n >= 2:
                    pe.wait_ge(g_sb, n - 1)
                pe.matmul(bank[n % 2][:], WqT[:, h, c * P:(c + 1) * P], kT[:], start=True,
                          stop=True).then_inc(g_mm, 1)
            pe.wait_ge(g_sb, C * H)

            with pe.Fori(0, B) as b:
                tile0 = b * T

                def turn_xn(t):
                    pe.wait_ge(xn_ready, tile0 + (t + 1))
                    if t >= 1:
                        pe.wait_ge(xnT_sb, tile0 + t)
                    for c in range(C):
                        last = pe.transpose(turn_bank[:, c * P:(c + 1) * P], xn[:, t % 2, c * P:(c + 1) * P], ident[:])
                    last.then_inc(xnT_mm, 1)

                def scores(t):
                    pe.wait_ge(xnT_sb, tile0 + (t + 1))
                    if t >= 2:
                        pe.wait_ge(shifted, tile0 + (t - 1))
                    else:
                        pe.wait_ge(vw_sb, b * 4 + 2 * (t + 1))
                    for half in range(2):
                        for c in range(C):
                            last = pe.matmul(score_banks[t % 2][:, half * 512:(half + 1) * 512], xnT[:, t % 2, c, :],
                                             G[:, c, half * 8:half * 8 + 8, bass.ds(b, 1), :].rearrange("p h o s -> p h (o s)"),
                                             start=(c == 0), stop=(c == C - 1))
                    last.then_inc(scores_mm, 1)

                def attend(t):
                    pe.wait_ge(attn_ready, tile0 + (t + 1))
                    if t >= 1:
                        pe.wait_ge(attnT_sb, tile0 + t)
                    for m in range(M):
                        last = pe.transpose(attnT_bank[:, m, :], attn[:, t % 2, m * P:(m + 1) * P], ident[:])
                    last.then_inc(attnT_mm, 1)
                    pe.wait_ge(attnT_sb, tile0 + (t + 1))
                    if t >= 1:
                        pe.wait_ge(x1_ready, tile0 + t)
                    for m in range(M):
                        last = pe.matmul(out_bank[:, 0:D], attnT[:, m, :], VW[:, m, :], start=(m == 0), stop=(m == M - 1))
                    last.then_inc(out_mm, 1)

                def turn_x2(t):
                    pe.wait_ge(x2_ready, tile0 + (t + 1))
                    if t == 0:
                        pe.wait_ge(xnT_sb, tile0 + T)
                    else:
                        pe.wait_ge(x2T_sb, tile0 + t)
                    for c in range(C):
                        last = pe.transpose(turn_bank[:, c * P:(c + 1) * P], x2[:, t, c * P:(c + 1) * P], ident[:])
                    last.then_inc(x2T_mm, 1)

                pe.wait_ge(vTb_ready, b + 1)
                turn_xn(0)
                for k in range(4):
                    for odd in range(2):
                        last = pe.matmul(score_banks[k // 2][64 * odd:64 * odd + SC, 512 * (k % 2):512 * (k % 2) + 512], vT_b[:],
                                         Wo[:, 4 * k + odd:4 * k + odd + 3:2, :], start=True, stop=True)
                    last.then_inc(vw_mm, 1)
                for t in range(T + 2):
                    if t < T:
                        scores(t)
                    if t + 1 < T:
                        turn_xn(t + 1)
                    if 1 <= t <= T:
                        attend(t - 1)
                    if t >= 2:
                        turn_x2(t - 2)

        @block.scalar
        def _(act):
            act.wait_ge(kv_mm, 1)
            act.mul(kT[:], bank[0][0:DK, :], float(DK) ** -0.5).then_inc(kv_sb, 1)
            act.wait_ge(kv_mm, 2)
            act.copy(vT[:].rearrange("p b s -> p (b s)"), bank[1][0:DK, :]).then_inc(kv_sb, 1)
            act.wait_ge(kv_sb, 2)
            for n in range(0, C * H):
                c, h = divmod(n, H)
                act.wait_ge(g_mm, n + 1)
                act.copy(G[:, c, h, :, :].rearrange("p b s -> p (b s)"), bank[n % 2][:]).then_inc(g_sb, 1)

            with act.Fori(0, B) as b:
                tile0 = b * T

                def take_xnT(t):
                    act.wait_ge(xnT_mm, tile0 + (t + 1))
                    if t >= 2:
                        act.wait_ge(scores_mm, tile0 + (t - 1))
                    act.copy(xnT[:, t % 2, :, :].rearrange("p c n -> p (c n)"), turn_bank[:, 0:D]).then_inc(xnT_sb, 1)

                act.copy(vT_b[:], vT[:, bass.ds(b, 1), :].rearrange("p o s -> p (o s)")).then_inc(vTb_ready, 1)
                take_xnT(0)
                for k in range(4):
                    act.wait_ge(vw_mm, b * 4 + (k + 1))
                    act.copy(VW[:, 2 * k:2 * k + 2, :].rearrange("p m d -> p (m d)"),
                             score_banks[k // 2][:, 512 * (k % 2):512 * (k % 2) + 512]).then_inc(vw_sb, 1)
                for t in range(T + 2):
                    if t + 1 < T:
                        take_xnT(t + 1)
                    if t < T:
                        act.wait_ge(shifted, tile0 + (t + 1))
                        act.activation(attn[:, t % 2, :], attn[:, t % 2, :], ACT.Exp).then_inc(exped, 1)
                    if 1 <= t <= T:
                        act.wait_ge(attnT_mm, tile0 + t)
                        if t >= 2:
                            act.wait_ge(out_mm, tile0 + (t - 1))
                        act.copy(attnT[:].rearrange("p m n -> p (m n)"),
                                 attnT_bank[:].rearrange("p m n -> p (m n)")).then_inc(attnT_sb, 1)
                    if t >= 2:
                        act.wait_ge(x2T_mm, tile0 + (t - 1))
                        if t == 2:
                            act.wait_ge(x2T_stored, b * DMA + DMA)
                        act.copy(x2T[:, :, (t - 2) * P:(t - 1) * P],
                                 turn_bank[:, 0:D].rearrange("p (c n) -> p c n", c=C)).then_inc(x2T_sb, 1)

        @block.gpsimd
        def _(pool):
            pool.memset(minus_half[:], -0.5).then_inc(half_set, 1)
            pool.memset(seen[:], 1.0).then_inc(half_set, 1)
            pool.memset(hidden[:], 0.0).then_inc(half_set, 1)
            pool.wait_ge(half_set, 3)
            pool.affine_select(out=seen[:], in_=seen[:], compare_op=ALU.is_ge, fill=0.0, base=0,
                               pattern=[[-1, SC]], channel_multiplier=1).then_inc(mask_set, 1)
            pool.affine_select(out=hidden[:], in_=hidden[:], compare_op=ALU.is_ge, fill=NEG, base=0,
                               pattern=[[-1, SC]], channel_multiplier=1).then_inc(mask_set, 1)
            with pool.Fori(0, B) as b:
                tile0 = b * T
                norms = [0]

                def inverse_root():
                    norms[0] += 1
                    pool.wait_ge(var_ready, b * (2 * T) + norms[0])
                    pool.tensor_tensor(rstd[:], var_eps[:], minus_half[:], ALU.pow).then_inc(rstd_ready, 1)

                inverse_root()
                for t in range(T + 2):
                    if t + 1 < T:
                        inverse_root()
                    if t >= 2:
                        inverse_root()
                    if t >= T:
                        continue
                    pool.wait_ge(rz_ready, tile0 + (t + 1))
                    a = attn[:, t % 2, :].rearrange("p (h s) -> p h s", h=H)
                    pool.tensor_tensor(a, a, rz[:, t % 2, :].unsqueeze(2).to_broadcast([P, H, SC]),
                                       ALU.mult).then_inc(attn_ready, 1)

        STEPS = T * 6 + 2

        @block.vector
        def _(dve):
            dve.wait_ge(mask_set, 2)
            dve.memset(spare[:], 0.0)
            with dve.Fori(0, B) as b:
                tile0 = b * T
                steps, norms = [0], [0]

                def step(ins):
                    steps[0] += 1
                    ins.then_inc(dve_step, 1)
                    dve.wait_ge(dve_step, b * STEPS + steps[0])

                def normalise(dst, src, ready):
                    step(dve.bn_stats(stats[:], src))
                    dve.memset(spare[:], 0.0)
                    step(dve.bn_aggr(mv[:], stats[:]))
                    dve.tensor_scalar(var_eps[:], mv[:, 1:2], EPS, None, ALU.add).then_inc(var_ready, 1)
                    norms[0] += 1
                    dve.wait_ge(rstd_ready, b * (2 * T) + norms[0])
                    dve.tensor_scalar(dst, src, mv[:, 0:1], rstd[:], ALU.subtract, ALU.mult).then_inc(ready, 1)

                def norm_x(t):
                    dve.wait_ge(x_in[t], b * DMA + DMA)
                    if t >= 2:
                        dve.wait_ge(xnT_mm, tile0 + (t - 1))
                    normalise(xn[:, t % 2, :], xt[:, t, :], xn_ready)
                    dve.wait_ge(xn_ready, tile0 + (t + 1))

                def shift(t):
                    a = attn[:, t % 2, :].rearrange("p (h s) -> p h s", h=H)
                    dve.wait_ge(scores_mm, tile0 + (t + 1))
                    if t == 0:
                        step(dve.tensor_tensor(a, score_banks[0][:].rearrange("p (h s) -> p h s", h=H),
                                               seen[:].unsqueeze(1).to_broadcast([P, H, SC]), ALU.mult))
                        step(dve.tensor_tensor(a, a, hidden[:].unsqueeze(1).to_broadcast([P, H, SC]), ALU.add))
                        src = a
                    else:
                        src = score_banks[t % 2][:].rearrange("p (h s) -> p h s", h=H)
                        if t >= 2:
                            dve.wait_ge(attnT_mm, tile0 + (t - 1))
                    step(dve.tensor_reduce(mx[:], src, X, ALU.max))
                    dve.tensor_tensor(a, src, mx[:].unsqueeze(2).to_broadcast([P, H, SC]),
                                      ALU.subtract).then_inc(shifted, 1)

                def sums(t):
                    dve.wait_ge(exped, tile0 + (t + 1))
                    step(dve.tensor_reduce(total[:], attn[:, t % 2, :].rearrange("p (h s) -> p h s", h=H), X, ALU.add))
                    if t >= 2:
                        dve.wait_ge(attn_ready, tile0 + (t - 1))
                    dve.reciprocal(rz[:, t % 2, :], total[:]).then_inc(rz_ready, 1)
                    dve.wait_ge(rz_ready, tile0 + (t + 1))

                def finish(t):
                    dve.wait_ge(out_mm, tile0 + (t + 1))
                    if t == 0:
                        dve.wait_ge(tiles_stored, b * (T * 2 * DMA) + DMA)
                    dve.tensor_tensor(x1[:, t, :], out_bank[:, 0:D], xt[:, t, :], ALU.add).then_inc(x1_ready, 1)
                    dve.wait_ge(x1_ready, tile0 + (t + 1))
                    normalise(x2[:, t, :], x1[:, t, :], x2_ready)
                    dve.wait_ge(x2_ready, tile0 + (t + 1))

                norm_x(0)
                for t in range(T + 2):
                    if t + 1 < T:
                        norm_x(t + 1)
                    if t < T:
                        shift(t)
                    if t >= 2:
                        finish(t - 2)
                    if t < T:
                        sums(t)
                dve.wait_ge(x2T_sb, tile0 + T)
                dve.tensor_reduce(colsum[:, :, bass.ds(b, 1)], x2T[:], X, ALU.add).then_inc(colsum_done, 1)
                assert steps[0] == STEPS


def gate(nc, dram, index_dram, weight_dram, keep):
    with ExitStack() as ctx:
        def sb(name, shape, dt=F32):
            return ctx.enter_context(nc.sbuf_tensor(name, shape, dt))

        logits_ps = ctx.enter_context(nc.psum_tensor("logits_ps", [B, E], F32))
        colsum, index, weight = keep["colsum"], keep["index"], keep["weight"]
        gwT, gb = sb("gwT", [P, C, E]), sb("gb", [B, E])
        before, number = sb("before", [B, E, E]), sb("number", [B, TOPK, E])
        slot_no = sb("slot_no", [B, TOPK, E])
        logit, prob, mx, total = sb("logit", [B, E]), sb("prob", [B, E]), sb("g_mx", [B, 1]), sb("g_total", [B, 1])
        wins, ties = sb("wins", [B, E, E]), sb("ties", [B, E, E])
        rank, chosen = sb("rank", [B, E]), sb("chosen", [B, TOPK, E])
        idx_f, idx_i, wts = sb("idx_f", [B, TOPK]), sb("idx_i", [B, TOPK], I32), sb("wts", [B, TOPK])
        loaded = ctx.enter_context(nc.semaphore("g_loaded"))
        logits_mm = ctx.enter_context(nc.semaphore("g_logits_mm"))
        step_done = ctx.enter_context(nc.semaphore("g_step_done"))
        exped = ctx.enter_context(nc.semaphore("g_exped"))
        stored = ctx.enter_context(nc.semaphore("g_stored"))
        PRE_EXP, ALL = 4, 18
        block = ctx.enter_context(nc.Block())

        @block.sync
        def _(sp):
            sp.dma_start(gwT[:], dram["gate_wT"].rearrange("(c p) e -> p c e", p=P)).then_inc(loaded, DMA)
            for dst, src in ((gb, dram["gate_b"]), (before, dram["before"]), (number, dram["number"]),
                             (slot_no, dram["slot_no"])):
                sp.dma_start(dst[:], src).then_inc(loaded, DMA)
            sp.wait_ge(step_done, ALL)
            sp.dma_start(index_dram.rearrange("(b k) -> b k", k=TOPK), idx_i[:]).then_inc(stored, DMA)
            sp.dma_start(weight_dram.rearrange("(b k) -> b k", k=TOPK), wts[:]).then_inc(stored, DMA)
            sp.wait_ge(stored, 2 * DMA)
            sp.dma_start(index[:], index_dram.unsqueeze(0)).then_inc(loaded, DMA)
            sp.dma_start(weight[:], weight_dram.unsqueeze(0).to_broadcast([P, PAIRS])).then_inc(loaded, DMA)
            sp.wait_ge(loaded, 7 * DMA)

        @block.tensor
        def _(pe):
            pe.wait_ge(loaded, 5 * DMA)
            for c in range(C):
                last = pe.matmul(logits_ps[:], colsum[:, c, :], gwT[:, c, :], start=(c == 0), stop=(c == C - 1))
            last.then_inc(logits_mm, 1)

        @block.scalar
        def _(act):
            act.wait_ge(step_done, PRE_EXP)
            act.activation(prob[:], prob[:], ACT.Exp).then_inc(exped, 1)

        @block.vector
        def _(dve):
            n = [0]

            def step(ins):
                n[0] += 1
                ins.then_inc(step_done, 1)
                dve.wait_ge(step_done, n[0])

            def over_f(a):
                return a[:].unsqueeze(1).to_broadcast([B, E, E])

            def over_e(a):
                return a[:].unsqueeze(2).to_broadcast([B, E, E])

            def over_k(a):
                return a[:].unsqueeze(1).to_broadcast([B, TOPK, E])

            dve.wait_ge(loaded, 5 * DMA)
            dve.wait_ge(logits_mm, 1)
            step(dve.tensor_scalar(logit[:], logits_ps[:], 1.0 / S, None, ALU.mult))
            step(dve.tensor_tensor(logit[:], logit[:], gb[:], ALU.add))
            step(dve.tensor_reduce(mx[:], logit[:], X, ALU.max))
            step(dve.tensor_scalar(prob[:], logit[:], mx[:], None, ALU.subtract))
            assert n[0] == PRE_EXP
            step(dve.tensor_tensor(wins[:], over_f(logit), over_e(logit), ALU.is_gt))
            step(dve.tensor_tensor(ties[:], over_f(logit), over_e(logit), ALU.is_equal))
            step(dve.tensor_tensor(ties[:], ties[:], before[:], ALU.mult))
            step(dve.tensor_tensor(wins[:], wins[:], ties[:], ALU.add))
            step(dve.tensor_reduce(rank[:], wins[:], X, ALU.add))
            step(dve.tensor_tensor(chosen[:], over_k(rank), slot_no[:], ALU.is_equal))
            step(dve.tensor_tensor(number[:], chosen[:], number[:], ALU.mult))
            step(dve.tensor_reduce(idx_f[:], number[:], X, ALU.add))
            step(dve.tensor_copy(idx_i[:], idx_f[:]))
            dve.wait_ge(exped, 1)
            step(dve.tensor_reduce(total[:], prob[:], X, ALU.add))
            step(dve.reciprocal(total[:], total[:]))
            step(dve.tensor_scalar(prob[:], prob[:], total[:], None, ALU.mult))
            step(dve.tensor_tensor(chosen[:], chosen[:], over_k(prob), ALU.mult))
            step(dve.tensor_reduce(wts[:], chosen[:], X, ALU.add))
            assert n[0] == ALL


HG = 4
GROUPS = H // HG
PT = H // 2
KQ = 3 * HD
SHIFT_ROW = KQ
KC = S // P
HALVES = GROUPS * KC * 2
UNITS = GROUPS * KC * HG
LEAD = 26
RING = 6


def stage_b(nc, dram, x2_dram, x2T_dram, qk_dram, out, keep):
    with ExitStack() as ctx:
        def sb(name, shape, dt=F32):
            return ctx.enter_context(nc.sbuf_tensor(name, shape, dt))

        def sem(name):
            return ctx.enter_context(nc.semaphore(name))

        bank = [ctx.enter_context(nc.psum_tensor(f"b_bank{n}", [P, 512], F32)) for n in range(2)]
        st_banks = [ctx.enter_context(nc.psum_tensor(f"b_st{n}", [P, 2, 512], F32)) for n in range(2)]
        o_bank = ctx.enter_context(nc.psum_tensor("b_o", [P, 512], F32))
        z_bank = ctx.enter_context(nc.psum_tensor("b_z", [P, 512], F32))
        mid = [st_banks[n // 2][:, n % 2, :] for n in range(4)]
        side = [o_bank, z_bank, bank[0], bank[1]]

        ident, index, weight = keep["ident"], keep["index"], keep["weight"]
        spread = sb("spread", [P, P])
        w_qkv = sb("w_qkv", [P, C, 3 * D])
        w_out = sb("w_out", [P, GROUPS, D])
        w_1 = sb("w_1", [P, C, F])
        w_2 = sb("w_2", [P, M, D])
        b_col = sb("b_col", [P, 4 + M])
        b_v = sb("b_v", [P, D])
        rows = sb("rows", [P, 5, D])
        x2T = sb("x2T_b", [P, C, S])
        x2 = sb("x2_b", [P, T, D])
        acc = sb("acc", [P, T, D])
        qk32 = sb("qk32", [P, 2, S])
        qk_parts = sb("qk_parts", [P, 4, 2, S], F32R)
        q_stack = sb("q_stack", [P, PT, S], F32R)
        k_stack = sb("k_stack", [P, PT, S], F32R)
        v_aug = sb("v_aug", [P, KC, H, 2 * HD])
        neg_max = sb("neg_max", [P, GROUPS, T, HG])
        shift = sb("shift", [HG, S], F32R)
        prob = sb("prob_b", [P, RING, 2, S])
        o_raw = sb("o_raw", [P, S])
        o_norm = sb("o_norm", [P, GROUPS, S])
        r = sb("r", [P, 2, D])
        y1 = sb("y1", [P, T, D])
        y1_b = sb("y1_b", [P, T, D])
        y1T = sb("y1T", [P, C, S])
        hidden = sb("hidden", [P, M, S])
        stats, mv, rstd = sb("stats_b", [P, 6]), sb("mv_b", [P, 2]), sb("rstd_b", [P, 1])
        var_eps, minus_half = sb("var_eps_b", [P, 1]), sb("minus_half_b", [P, 1])
        rz = sb("rz_b", [P, S])
        spare, spare_pool = sb("spare_b", [P, 1]), sb("spare_pool", [P, 1])
        w_pair = sb("w_pair", [P, 1])

        consts_in, zeros_set = sem("b_consts_in"), sem("b_zeros_set")
        qkv_in, x2T_in = sem("b_qkv_in"), sem("b_x2T_in")
        x2_in, acc_in = sem("b_x2_in"), sem("b_acc_in")
        w_out_in, w_1_in, w_2_in = sem("b_w_out_in"), sem("b_w_1_in"), sem("b_w_2_in")
        qk_mm, qk_full, qk_high, qk_low = sem("b_qk_mm"), sem("b_qk_full"), sem("b_qk_high"), sem("b_qk_low")
        qk_out, stacks_in = [sem(f"b_qk_out{u}") for u in range(4)], sem("b_stacks_in")
        v_mm, v_ready = sem("b_v_mm"), sem("b_v_ready")
        max_mm, max_done = sem("b_max_mm"), sem("b_max_done")
        shift_mm, shift_sb, shift_in = sem("b_shift_mm"), sem("b_shift_sb"), sem("b_shift_in")
        st_mm, prob_ready, pv_mm = sem("b_st_mm"), sem("b_prob_ready"), sem("b_pv_mm")
        o_sb, z_mm, o_ready = sem("b_o_sb"), sem("b_z_mm"), sem("b_o_ready")
        proj_mm, r_ready, y1_ready = sem("b_proj_mm"), sem("b_r_ready"), sem("b_y1_ready")
        y1b_ready = sem("b_y1b_ready")
        y1T_mm, y1T_sb = sem("b_y1T_mm"), sem("b_y1T_sb")
        hid_mm, hid_act, hid_dve = sem("b_hid_mm"), sem("b_hid_act"), sem("b_hid_dve")
        ff_mm, ff_taken, acc_ready, stored = sem("b_ff_mm"), sem("b_ff_taken"), sem("b_acc_ready"), sem("b_stored")
        half_set, var_ready, rstd_ready = sem("b_half_set"), sem("b_var_ready"), sem("b_rstd_ready")
        dve_step = sem("b_dve_step")

        block = ctx.enter_context(nc.Block())

        @block.sync
        def _(sp):
            def expert_of(i):
                return sp.value_load(index[:, bass.ds(i, 1)], min_val=0, max_val=E - 1)

            def whole(src, e):
                return src[bass.ds(e, 1)]

            def load_qkv(e, batch):
                sp.dma_start(w_qkv[:], whole(dram["w_qkv"], e).rearrange("o p c n -> p (o c) n")).then_inc(qkv_in, DMA)
                sp.dma_start(b_col[:], whole(dram["b_col"], e).rearrange("o p n -> p (o n)")).then_inc(qkv_in, DMA)
                sp.dma_start(b_v[:], whole(dram["b_v"], e).to_broadcast([P, D])).then_inc(qkv_in, DMA)
                sp.dma_start(x2T[:], x2T_dram[bass.ds(batch, 1)].rearrange("o p c n -> p (o c) n")).then_inc(x2T_in, DMA)

            def load_w_out(e):
                for j in range(HG):
                    sp.dma_start(w_out[32 * j:32 * j + HD, :, :],
                                 whole(dram["w_out"], e)[:, j].rearrange("o p g n -> p (o g) n")).then_inc(w_out_in, DMA)
                sp.dma_start(w_out[HD:HD + 1, 0, :], whole(dram["b_out"], e)).then_inc(w_out_in, DMA)

            def load_w_1(e):
                sp.dma_start(w_1[:], whole(dram["w_1"], e).rearrange("o p c n -> p (o c) n")).then_inc(w_1_in, DMA)

            def load_w_2(e):
                sp.dma_start(w_2[:], whole(dram["w_2"], e).rearrange("o p m n -> p (o m) n")).then_inc(w_2_in, DMA)
                sp.dma_start(rows[:], whole(dram["rows"], e).to_broadcast([P, 5, D])).then_inc(w_2_in, DMA)

            sp.dma_start(spread[:], dram["spread"]).then_inc(consts_in, DMA)
            sp.wait_ge(zeros_set, 2)
            first = expert_of(0)
            load_qkv(first, 0)
            load_w_out(first)
            load_w_1(first)
            load_w_2(first)

            def pair(i, prefetch):
                for u in range(4):
                    sp.wait_ge(qk_high, i * 4 + (u + 1))
                    sp.wait_ge(qk_low, i * 4 + (u + 1))
                    sp.dma_start(qk_dram[u], qk_parts[:, u, :, :].bitcast(F32)).then_inc(qk_out[u], DMA)
                for u in range(4):
                    sp.wait_ge(qk_out[u], i * DMA + DMA)
                    odd = u % 2
                    stack, order = (q_stack, (0, 0, 1)) if u < 2 else (k_stack, (0, 1, 0))
                    for n, part in enumerate(order):
                        row = 64 * odd + HD * n
                        sp.dma_start(stack[row:row + HD, :, :].bitcast(F32),
                                     qk_dram[u, :, part, :].rearrange("(m p) n -> p m n", p=HD)).then_inc(stacks_in, DMA)
                batch = i // TOPK
                sp.dma_start(x2[:], x2_dram[bass.ds(batch, 1)].rearrange("o (t p) d -> p (o t) d", p=P)).then_inc(x2_in, DMA)
                sp.dma_start(acc[:], out[bass.ds(batch, 1)].rearrange("o (t p) d -> p (o t) d", p=P)).then_inc(acc_in, DMA)
                if prefetch:
                    e = expert_of(i + 1)
                    sp.wait_ge(v_ready, i * T + T)
                for g in range(GROUPS):
                    sp.wait_ge(shift_sb, i * GROUPS + (g + 1))
                    for j in range(HG):
                        row = 64 * (j % 2) + SHIFT_ROW
                        sp.dma_start(q_stack[row:row + 1, 2 * g + j // 2, :].bitcast(F32),
                                     shift[j:j + 1, :].bitcast(F32)).then_inc(shift_in, DMA)
                if prefetch:
                    sp.wait_ge(proj_mm, i * T + T)
                    load_w_out(e)
                    sp.wait_ge(hid_mm, i * M + M)
                    sp.wait_ge(hid_act, i * (M // 2) + M // 2)
                    sp.wait_ge(hid_dve, i * (M // 2) + M // 2)
                    load_qkv(e, (i + 1) // TOPK)
                    load_w_1(e)
                for t in range(T):
                    sp.wait_ge(acc_ready, i * T + (t + 1))
                    sp.dma_start(out[bass.ds(batch, 1), t * P:(t + 1) * P, :].rearrange("o p d -> p (o d)"),
                                 acc[:, t, :]).then_inc(stored, DMA)
                sp.wait_ge(stored, i * (T * DMA) + T * DMA)
                if prefetch:
                    load_w_2(e)

            with sp.Fori(0, PAIRS - 1) as i:
                pair(i, True)
            pair(PAIRS - 1, False)

        @block.tensor
        def _(pe):
            pe.wait_ge(zeros_set, 3)
            pe.wait_ge(consts_in, DMA)
            with pe.Fori(0, PAIRS) as i:
                pe.wait_ge(qkv_in, i * (3 * DMA) + 3 * DMA)
                pe.wait_ge(x2T_in, i * DMA + DMA)
                for u in range(4):
                    for c in range(C):
                        last = pe.matmul(mid[u], w_qkv[:, c, u * P:(u + 1) * P], x2T[:, c, :], start=(c == 0), stop=(c == C - 1))
                    last.then_inc(qk_mm, 1)
                pe.wait_ge(qk_full, i * 4 + 1)
                for t in range(T):
                    for c in range(C):
                        last = pe.matmul(side[t][:, 0:D], x2T[:, c, t * P:(t + 1) * P], w_qkv[:, c, 2 * D:3 * D],
                                         start=(c == 0), stop=(c == C - 1))
                    last.then_inc(v_mm, 1)
                pe.wait_ge(v_ready, i * T + T)

                def stack_rows(h, extra):
                    first = 64 * (h % 2)
                    return slice(first, first + KQ + extra)

                def max_unit(u):
                    g, qc, j = u // 16, u % 16 // 4, u % 4
                    h = HG * g + j
                    if u >= 2:
                        pe.wait_ge(max_done, i * UNITS + (u - 1))
                    pe.matmul(bank[u % 2][:], q_stack[stack_rows(h, 0), h // 2, qc * P:(qc + 1) * P],
                              k_stack[stack_rows(h, 0), h // 2, :], start=True, stop=True).then_inc(max_mm, 1)

                def turn_max(g):
                    pe.wait_ge(max_done, i * UNITS + 16 * (g + 1))
                    if g == GROUPS - 1:
                        pe.wait_ge(o_ready, i * GROUPS + 1)
                    for qc in range(T):
                        last = pe.transpose(z_bank[0:HG, qc * P:(qc + 1) * P], neg_max[:, g, qc, :], ident[:])
                    last.then_inc(shift_mm, 1)

                def score_half(s):
                    g, kc, half = s // 8, s % 8 // 2, s % 2
                    if s >= 2:
                        pe.wait_ge(prob_ready, i * HALVES + (s - 1))
                    else:
                        pe.wait_ge(qk_full, i * 4 + 4)
                    for n in range(2):
                        h = HG * g + 2 * half + n
                        last = pe.matmul(st_banks[s % 2][:, n, :], k_stack[stack_rows(h, 1), h // 2, kc * P:(kc + 1) * P],
                                         q_stack[stack_rows(h, 1), h // 2, :], start=True, stop=True)
                    last.then_inc(st_mm, 1)

                def times_v(s):
                    g, kc = s // 8, s % 8 // 2
                    pe.wait_ge(prob_ready, i * HALVES + (s + 1))
                    if kc == 0 and g >= 1:
                        pe.wait_ge(o_sb, i * GROUPS + g)
                    for j in range(HG):
                        last = pe.matmul(o_bank[32 * j:32 * j + 32, :], v_aug[:, kc, HG * g + j, :],
                                         prob[:, (s - 1 + j // 2) % RING, j % 2, :], start=(kc == 0), stop=(kc == KC - 1))
                    last.then_inc(pv_mm, 1)

                def spread_sums(g):
                    pe.wait_ge(o_sb, i * GROUPS + (g + 1))
                    pe.wait_ge(shift_sb, i * GROUPS + min(g + 3, GROUPS))
                    if g >= 1:
                        pe.wait_ge(o_ready, i * GROUPS + g)
                    pe.matmul(z_bank[:], spread[:], o_raw[:], start=True, stop=True).then_inc(z_mm, 1)

                pe.wait_ge(stacks_in, i * (12 * DMA) + 12 * DMA)
                for u in range(LEAD):
                    max_unit(u)
                turn_max(0)
                for s in range(HALVES):
                    if s % 8 == 0:
                        pe.wait_ge(shift_in, i * (H * DMA) + (s // 8 + 1) * (HG * DMA))
                    score_half(s)
                    for u in range(LEAD + 2 * s, min(LEAD + 2 * s + 2, UNITS)):
                        max_unit(u)
                    if s % 8 == 5 and s // 8 >= 1:
                        spread_sums(s // 8 - 1)
                    if s % 8 == 3 and s // 8 + 1 < GROUPS:
                        turn_max(s // 8 + 1)
                    if s % 2 == 1 and s >= 3:
                        times_v(s - 2)
                times_v(HALVES - 1)
                spread_sums(GROUPS - 1)

                pe.wait_ge(w_out_in, i * (5 * DMA) + 5 * DMA)
                pe.wait_ge(o_ready, i * GROUPS + GROUPS)
                for t in range(T):
                    for g in range(GROUPS):
                        last = pe.matmul(mid[t][:, 0:D], o_norm[:, g, t * P:(t + 1) * P], w_out[:, g, :],
                                         start=(g == 0), stop=(g == GROUPS - 1))
                    last.then_inc(proj_mm, 1)
                for t in range(T):
                    pe.wait_ge(y1_ready, i * T + (t + 1))
                    if t >= 2:
                        pe.wait_ge(y1T_sb, i * T + (t - 1))
                    for c in range(C):
                        last = pe.transpose(bank[t % 2][:, c * P:(c + 1) * P], y1[:, t, c * P:(c + 1) * P], ident[:])
                    last.then_inc(y1T_mm, 1)
                pe.wait_ge(y1T_sb, i * T + T)
                pe.wait_ge(w_1_in, i * DMA + DMA)
                for m in range(M):
                    if m >= 4:
                        if m % 2 == 0:
                            pe.wait_ge(hid_act, i * (M // 2) + (m // 2 - 1))
                        else:
                            pe.wait_ge(hid_dve, i * (M // 2) + (m // 2 - 1))
                    for c in range(C):
                        last = pe.matmul(mid[m % 4], w_1[:, c, m * P:(m + 1) * P], y1T[:, c, :], start=(c == 0), stop=(c == C - 1))
                    last.then_inc(hid_mm, 1)
                pe.wait_ge(w_2_in, i * (2 * DMA) + 2 * DMA)
                pe.wait_ge(hid_act, i * (M // 2) + M // 2)
                pe.wait_ge(hid_dve, i * (M // 2) + M // 2)
                for t in range(T):
                    for m in range(M):
                        last = pe.matmul(side[t][:, 0:D], hidden[:, m, t * P:(t + 1) * P], w_2[:, m, :],
                                         start=(m == 0), stop=(m == M - 1))
                    last.then_inc(ff_mm, 1)

        @block.scalar
        def _(act):
            with act.Fori(0, PAIRS) as i:
                for u in range(4):
                    act.wait_ge(qk_full, i * 4 + (u + 1))
                    act.copy(qk_parts[:, u, 0, :], qk32[:, u % 2, :]).then_inc(qk_high, 1)

                def take_shift(g):
                    act.wait_ge(shift_mm, i * GROUPS + (g + 1))
                    if g >= 1:
                        act.wait_ge(shift_in, i * (H * DMA) + g * (HG * DMA))
                    act.copy(shift[:], z_bank[0:HG, :]).then_inc(shift_sb, 1)

                def take_o(g):
                    act.wait_ge(pv_mm, i * (GROUPS * KC) + (g + 1) * KC)
                    if g >= 1:
                        act.wait_ge(z_mm, i * GROUPS + g)
                        act.wait_ge(o_ready, i * GROUPS + g)
                    act.copy(o_raw[:], o_bank[:]).then_inc(o_sb, 1)

                take_shift(0)
                for s in range(HALVES):
                    act.wait_ge(st_mm, i * HALVES + (s + 1))
                    if s >= RING:
                        act.wait_ge(pv_mm, i * (GROUPS * KC) + (s - RING) // 2 + 1)
                    act.activation(prob[:, s % RING, :, :].rearrange("p n q -> p (n q)"),
                                   st_banks[s % 2][:].rearrange("p n q -> p (n q)"), ACT.Exp).then_inc(prob_ready, 1)
                    if s % 8 == 3 and s // 8 + 1 < GROUPS:
                        take_shift(s // 8 + 1)
                    if s % 8 == 1 and s // 8 >= 1:
                        take_o(s // 8 - 1)
                take_o(GROUPS - 1)
                for t in range(T):
                    act.wait_ge(y1T_mm, i * T + (t + 1))
                    act.copy(y1T[:, :, t * P:(t + 1) * P], bank[t % 2][:, 0:D].rearrange("p (c n) -> p c n", c=C)).then_inc(y1T_sb, 1)
                for m in range(0, M, 2):
                    act.wait_ge(hid_mm, i * M + (m + 1))
                    act.activation(hidden[:, m, :], mid[m % 4], ACT.Relu, bias=b_col[:, 4 + m:5 + m]).then_inc(hid_act, 1)

        @block.gpsimd
        def _(pool):
            pool.memset(minus_half[:], -0.5).then_inc(half_set, 1)
            pool.wait_ge(half_set, 1)
            pool.memset(spare_pool[:], 0.0)
            with pool.Fori(0, PAIRS) as i:
                for u in range(4):
                    pool.wait_ge(qk_high, i * 4 + (u + 1))
                    pool.tensor_tensor(qk_parts[:, u, 1, :], qk32[:, u % 2, :], qk_parts[:, u, 0, :].bitcast(F32),
                                       ALU.subtract).then_inc(qk_low, 1)

                def inverse_root(n):
                    pool.wait_ge(var_ready, i * (2 * T) + (n + 1))
                    pool.tensor_tensor(rstd[:], var_eps[:], minus_half[:], ALU.pow).then_inc(rstd_ready, 1)

                inverse_root(0)
                for t in range(T):
                    if t + 1 < T:
                        inverse_root(t + 1)
                    pool.wait_ge(y1_ready, i * T + (t + 1))
                    pool.tensor_tensor(y1_b[:, t, :], y1[:, t, :], rows[:, 0, :], ALU.add).then_inc(y1b_ready, 1)
                for t in range(T):
                    inverse_root(T + t)

        MID_STEPS = GROUPS + T * 4 + T * 5 + 1

        @block.vector
        def _(dve):
            dve.memset(w_out[:], 0.0).then_inc(zeros_set, 1)
            dve.memset(k_stack[:].bitcast(F32), 1.0).then_inc(zeros_set, 1)
            dve.memset(v_aug[:], 1.0).then_inc(zeros_set, 1)
            dve.wait_ge(zeros_set, 3)
            with dve.Fori(0, PAIRS) as i:
                steps, norms = [0], [0]

                def step(ins):
                    steps[0] += 1
                    ins.then_inc(dve_step, 1)
                    dve.wait_ge(dve_step, i * MID_STEPS + steps[0])

                dve.wait_ge(qkv_in, i * (3 * DMA) + 3 * DMA)
                for u in range(4):
                    dve.wait_ge(qk_mm, i * 4 + (u + 1))
                    if u >= 2:
                        dve.wait_ge(qk_low, i * 4 + (u - 1))
                    dve.tensor_scalar(qk32[:, u % 2, :], mid[u], b_col[:, u:u + 1], float(HD) ** -0.5 if u < 2 else 1.0,
                                      ALU.add, ALU.mult).then_inc(qk_full, 1)
                for t in range(T):
                    dve.wait_ge(v_mm, i * T + (t + 1))
                    dve.tensor_tensor(v_aug[:, t, :, 0:HD], side[t][:, 0:D].rearrange("p (h d) -> p h d", h=H),
                                      b_v[:].rearrange("p (h d) -> p h d", h=H), ALU.add).then_inc(v_ready, 1)

                def divide(g):
                    dve.wait_ge(z_mm, i * GROUPS + (g + 1))
                    step(dve.reciprocal(rz[:], z_bank[:]))
                    dve.tensor_tensor(o_norm[:, g, :], o_raw[:], rz[:], ALU.mult).then_inc(o_ready, 1)
                    dve.wait_ge(o_ready, i * GROUPS + (g + 1))

                for u in range(UNITS):
                    g, qc, j = u // 16, u % 16 // 4, u % 4
                    dve.wait_ge(max_mm, i * UNITS + (u + 1))
                    dve.tensor_reduce(neg_max[:, g, qc, j:j + 1], bank[u % 2][:], X, ALU.max, negate=True).then_inc(max_done, 1)
                    if u == LEAD + 27:
                        divide(0)
                for g in range(1, GROUPS):
                    divide(g)

                def normalise(src, dst):
                    step(dve.bn_stats(stats[:], src))
                    dve.memset(spare[:], 0.0)
                    step(dve.bn_aggr(mv[:], stats[:]))
                    dve.tensor_scalar(var_eps[:], mv[:, 1:2], EPS, None, ALU.add).then_inc(var_ready, 1)
                    norms[0] += 1
                    dve.wait_ge(rstd_ready, i * (2 * T) + norms[0])
                    step(dve.tensor_scalar(dst, src, mv[:, 0:1], rstd[:], ALU.subtract, ALU.mult))

                dve.wait_ge(w_2_in, i * (2 * DMA) + 2 * DMA)
                dve.wait_ge(x2_in, i * DMA + DMA)
                for t in range(T):
                    dve.wait_ge(proj_mm, i * T + (t + 1))
                    rt = r[:, t % 2, :]
                    dve.tensor_tensor(rt, mid[t][:, 0:D], x2[:, t, :], ALU.add).then_inc(r_ready, 1)
                    dve.wait_ge(r_ready, i * T + (t + 1))
                    normalise(rt, rt)
                    step(dve.tensor_tensor(rt, rt, rows[:, 1, :], ALU.mult))
                    dve.tensor_tensor(y1[:, t, :], rt, rows[:, 2, :], ALU.add).then_inc(y1_ready, 1)
                dve.tensor_copy(w_pair[:], weight[:, bass.ds(i, 1)]).then_inc(dve_step, 1)
                steps[0] += 1
                dve.wait_ge(dve_step, i * MID_STEPS + steps[0])
                dve.wait_ge(y1_ready, i * T + T)
                for m in range(1, M, 2):
                    dve.wait_ge(hid_mm, i * M + (m + 1))
                    dve.tensor_scalar(hidden[:, m, :], mid[m % 4], b_col[:, 4 + m:5 + m], 0.0, ALU.add, ALU.max).then_inc(hid_dve, 1)
                dve.wait_ge(acc_in, i * DMA + DMA)
                for t in range(T):
                    dve.wait_ge(ff_mm, i * T + (t + 1))
                    dve.wait_ge(y1b_ready, i * T + (t + 1))
                    rt = r[:, t % 2, :]
                    dve.tensor_tensor(rt, side[t][:, 0:D], y1_b[:, t, :], ALU.add).then_inc(ff_taken, 1)
                    dve.wait_ge(ff_taken, i * T + (t + 1))
                    normalise(rt, rt)
                    step(dve.tensor_tensor(rt, rt, rows[:, 3, :], ALU.mult))
                    step(dve.tensor_tensor(rt, rt, rows[:, 4, :], ALU.add))
                    dve.scalar_tensor_tensor(out=acc[:, t, :], in0=rt, scalar=w_pair[:], in1=acc[:, t, :],
                                             op0=ALU.mult, op1=ALU.add).then_inc(acc_ready, 1)
                    dve.wait_ge(acc_ready, i * T + (t + 1))
                assert steps[0] == MID_STEPS, steps


def build(nc, dram, out):
    x2_dram = nc.dram_tensor("x2_scratch", (B, S, D), F32, kind="Internal").ap()
    x2T_dram = nc.dram_tensor("x2T_scratch", (B, P, C, S), F32, kind="Internal").ap()
    qk_dram = nc.dram_tensor("qk_scratch", (4, P, 2, S), F32, kind="Internal").ap()
    index_dram = nc.dram_tensor("index_scratch", (PAIRS,), I32, kind="Internal").ap()
    weight_dram = nc.dram_tensor("weight_scratch", (PAIRS,), F32, kind="Internal").ap()
    with ExitStack() as ctx:
        keep = {name: ctx.enter_context(nc.sbuf_tensor(name, shape, dt)) for name, shape, dt in (
            ("ident", [P, P], F32), ("colsum", [P, C, B], F32), ("index", [1, PAIRS], I32), ("weight", [P, PAIRS], F32))}
        stage_a(nc, dram, x2_dram, x2T_dram, out, keep)
        gate(nc, dram, index_dram, weight_dram, keep)
        stage_b(nc, dram, x2_dram, x2T_dram, qk_dram, out, keep)


def kernel(**inputs):
    import numpy as np
    import concourse.bacc as bacc
    from concourse.bass_utils import run_bass_kernel_spmd

    def arr(name):
        return np.asarray(inputs[name])

    iw, ib = arr("L0_ffn_in_proj_w"), arr("L0_ffn_in_proj_b")

    def even_odd(a):
        return a.reshape(E, PT, 2, HD, -1).transpose(0, 2, 1, 3, 4).reshape(E, D, -1)

    qkv = np.concatenate([even_odd(iw[:, 0:D]), even_odd(iw[:, D:2 * D]), iw[:, 2 * D:]], axis=1)
    b_qk = np.concatenate([even_odd(ib[:, 0:D]), even_odd(ib[:, D:2 * D])], axis=1).reshape(E, 4, P)
    k = np.arange(P)
    e = np.arange(E)
    arrays = {
        "x": arr("x"),
        "ctxT": arr("ctx_1024").reshape(B * SC, D).T,
        "Wk": arr("L0_xattn_W_k"), "Wv": arr("L0_xattn_W_v"),
        "WqT": arr("L0_xattn_W_q").reshape(D, H, DK).transpose(2, 1, 0),
        "Wo": arr("L0_xattn_W_o").reshape(H, DK, D).transpose(1, 0, 2),
        "gate_wT": arr("L0_ffn_gate_w").T,
        "gate_b": np.broadcast_to(arr("L0_ffn_gate_b"), (B, E)),
        "w_qkv": qkv.reshape(E, 3 * D, C, P).transpose(0, 3, 2, 1),
        "b_col": np.concatenate([b_qk, arr("L0_ffn_lin1_b").reshape(E, M, P)], axis=1).transpose(0, 2, 1),
        "b_v": ib[:, 2 * D:],
        "w_out": arr("L0_ffn_out_proj_w").reshape(E, D, GROUPS, HG, HD).transpose(0, 3, 4, 2, 1),
        "b_out": arr("L0_ffn_out_proj_b"),
        "w_1": arr("L0_ffn_lin1_w").reshape(E, F, C, P).transpose(0, 3, 2, 1),
        "w_2": arr("L0_ffn_lin2_w").reshape(E, D, M, P).transpose(0, 3, 2, 1),
        "rows": np.stack([arr("L0_ffn_" + n) for n in ("lin2_b", "ln1_w", "ln1_b", "ln2_w", "ln2_b")], axis=1),
        "ident": np.eye(P, dtype=np.float32),
        "spread": (k[:, None] == 32 * (k[None, :] // 32) + HD).astype(np.float32),
        "before": np.broadcast_to(e[None, :] < e[:, None], (B, E, E)).astype(np.float32),
        "number": np.broadcast_to(e, (B, TOPK, E)).astype(np.float32),
        "slot_no": np.broadcast_to(np.arange(TOPK)[:, None], (B, TOPK, E)).astype(np.float32),
    }
    nc = bacc.Bacc("TRN2", target_bir_lowering=False, num_devices=1)
    arrays = {f"in_{n}": np.ascontiguousarray(a) for n, a in arrays.items()}
    dram = {n[3:]: nc.dram_tensor(n, a.shape, mybir.dt.from_np(a.dtype), kind="ExternalInput").ap()
            for n, a in arrays.items()}
    out = nc.dram_tensor("out", (B, S, D), F32, kind="ExternalOutput").ap()
    build(nc, dram, out)
    r = run_bass_kernel_spmd(nc, [arrays], core_ids=[0])
    return r.results[0]["out"]
```

```python
from contextlib import ExitStack

import concourse.bass as bass
from concourse import mybir

ALU = mybir.AluOpType
ACT = mybir.ActivationFunctionType
X = mybir.AxisListType.X
F32 = mybir.dt.float32
F32R = mybir.dt.float32r
I32 = mybir.dt.int32

P = 128
B, S, D = 8, 512, 256
T = S // P
C = D // P
SC = 64
H = 16
DK = 64
HD = D // H
E = 4
TOPK = 2
PAIRS = B * TOPK
F = 1024
M = F // P
EPS = 1e-5
NEG = -1e9
DMA = 16


def stage_a(nc, dram, x2_dram, x2T_dram, out, keep):
    with ExitStack() as ctx:
        def sb(name, shape, dt=F32):
            return ctx.enter_context(nc.sbuf_tensor(name, shape, dt))

        def sem(name):
            return ctx.enter_context(nc.semaphore(name))

        bank = [ctx.enter_context(nc.psum_tensor(f"a_bank{n}", [P, 512], F32)) for n in range(6, 8)]
        score_banks = [ctx.enter_context(nc.psum_tensor(f"a_scores{n}", [P, H * SC], F32)) for n in range(2)]
        attnT_bank = ctx.enter_context(nc.psum_tensor("a_attnT", [P, M, P], F32))
        turn_bank, out_bank = bank

        ident, colsum = keep["ident"], keep["colsum"]
        ctxT = sb("ctxT", [P, C, B * SC])
        Wk = sb("Wk", [P, C, DK])
        Wv = sb("Wv", [P, C, DK])
        WqT = sb("WqT", [DK, H, D])
        Wo = sb("Wo", [DK, H, D])
        kT = sb("kT", [DK, B * SC])
        vT = sb("vT", [DK, B, SC])
        vT_b = sb("vT_b", [DK, SC])
        G = sb("G", [P, C, H, B, SC])
        VW = sb("VW", [P, M, D])
        xt = sb("xt", [P, T, D])
        xn = sb("xn", [P, 2, D])
        xnT = sb("xnT", [P, 2, C, P])
        attn = sb("attn", [P, 2, H * SC])
        attnT = sb("attnT", [P, M, P])
        x1 = sb("x1", [P, T, D])
        x2 = sb("x2", [P, T, D])
        x2T = sb("x2T_a", [P, C, S])
        stats = sb("stats_a", [P, 6])
        mv = sb("mv_a", [P, 2])
        rstd = sb("rstd_a", [P, 1])
        spare = sb("spare_a", [P, 1])
        seen, hidden = sb("seen", [P, SC]), sb("hidden_a", [P, SC])
        var_eps = sb("var_eps_a", [P, 1])
        minus_half = sb("minus_half_a", [P, 1])
        mx = sb("mx", [P, H])
        total = sb("total", [P, H])
        rz = sb("rz", [P, 2, H])

        consts_in = sem("a_consts_in")
        x_in = [sem(f"a_x_in{t}") for t in range(T)]
        kv_mm, kv_sb = sem("a_kv_mm"), sem("a_kv_sb")
        g_mm, g_sb = sem("a_g_mm"), sem("a_g_sb")
        vTb_ready = sem("a_vTb_ready")
        vw_mm, vw_sb = sem("a_vw_mm"), sem("a_vw_sb")
        xn_ready, xnT_mm, xnT_sb = sem("a_xn_ready"), sem("a_xnT_mm"), sem("a_xnT_sb")
        scores_mm = sem("a_scores_mm")
        mask_set = sem("a_mask_set")
        shifted, exped = sem("a_shifted"), sem("a_exped")
        rz_ready, attn_ready = sem("a_rz_ready"), sem("a_attn_ready")
        attnT_mm, attnT_sb = sem("a_attnT_mm"), sem("a_attnT_sb")
        out_mm, x1_ready, x2_ready = sem("a_out_mm"), sem("a_x1_ready"), sem("a_x2_ready")
        x2T_mm, x2T_sb = sem("a_x2T_mm"), sem("a_x2T_sb")
        colsum_done = sem("a_colsum_done")
        tiles_stored, x2T_stored = sem("a_tiles_stored"), sem("a_x2T_stored")
        half_set, var_ready, rstd_ready = sem("a_half_set"), sem("a_var_ready"), sem("a_rstd_ready")
        dve_step = sem("a_dve_step")

        block = ctx.enter_context(nc.Block())

        @block.sync
        def _(sp):
            sp.sem_inc(tiles_stored, DMA)
            sp.sem_inc(x2T_stored, DMA)
            for dst, src in ((ctxT, dram["ctxT"].rearrange("(c p) n -> p c n", p=P)),
                             (Wk, dram["Wk"].rearrange("(c p) n -> p c n", p=P)),
                             (Wv, dram["Wv"].rearrange("(c p) n -> p c n", p=P)),
                             (WqT, dram["WqT"]), (Wo, dram["Wo"]), (ident, dram["ident"])):
                sp.dma_start(dst[:], src).then_inc(consts_in, DMA)
            for t in range(T):
                sp.dma_start(xt[:, t, :], dram["x"][0, t * P:(t + 1) * P, :]).then_inc(x_in[t], DMA)

            def finish_batch(b, prefetch):
                for t in range(T):
                    rows = slice(t * P, (t + 1) * P)
                    sp.wait_ge(x2_ready, b * T + (t + 1))
                    sp.dma_start(out[bass.ds(b, 1), rows, :].rearrange("o p d -> p (o d)"),
                                 x1[:, t, :]).then_inc(tiles_stored, DMA)
                    sp.dma_start(x2_dram[bass.ds(b, 1), rows, :].rearrange("o p d -> p (o d)"),
                                 x2[:, t, :]).then_inc(tiles_stored, DMA)
                    if prefetch:
                        sp.dma_start(xt[:, t, :], dram["x"][bass.ds(b + 1, 1), rows, :].rearrange(
                            "o p d -> p (o d)")).then_inc(x_in[t], DMA)
                sp.wait_ge(x2T_sb, b * T + T)
                sp.dma_start(x2T_dram[bass.ds(b, 1), :, :, :].rearrange("o p c n -> p (o c) n"),
                             x2T[:]).then_inc(x2T_stored, DMA)

            with sp.Fori(0, B - 1) as b:
                finish_batch(b, True)
            finish_batch(B - 1, False)
            sp.wait_ge(tiles_stored, B * T * 2 * DMA + DMA)
            sp.wait_ge(x2T_stored, B * DMA + DMA)

        @block.tensor
        def _(pe):
            pe.wait_ge(consts_in, 6 * DMA)
            for n, w in enumerate((Wk, Wv)):
                for c in range(C):
                    last = pe.matmul(bank[n][0:DK, :], w[:, c, :], ctxT[:, c, :], start=(c == 0), stop=(c == C - 1))
                last.then_inc(kv_mm, 1)
            pe.wait_ge(kv_sb, 2)
            for n in range(C * H):
                c, h = divmod(n, H)
                if n >= 2:
                    pe.wait_ge(g_sb, n - 1)
                pe.matmul(bank[n % 2][:], WqT[:, h, c * P:(c + 1) * P], kT[:], start=True,
                          stop=True).then_inc(g_mm, 1)
            pe.wait_ge(g_sb, C * H)

            with pe.Fori(0, B) as b:
                tile0 = b * T

                def turn_xn(t):
                    pe.wait_ge(xn_ready, tile0 + (t + 1))
                    if t >= 1:
                        pe.wait_ge(xnT_sb, tile0 + t)
                    for c in range(C):
                        last = pe.transpose(turn_bank[:, c * P:(c + 1) * P], xn[:, t % 2, c * P:(c + 1) * P], ident[:])
                    last.then_inc(xnT_mm, 1)

                def scores(t):
                    pe.wait_ge(xnT_sb, tile0 + (t + 1))
                    if t >= 2:
                        pe.wait_ge(shifted, tile0 + (t - 1))
                    else:
                        pe.wait_ge(vw_sb, b * 4 + 2 * (t + 1))
                    for half in range(2):
                        for c in range(C):
                            last = pe.matmul(score_banks[t % 2][:, half * 512:(half + 1) * 512], xnT[:, t % 2, c, :],
                                             G[:, c, half * 8:half * 8 + 8, bass.ds(b, 1), :].rearrange("p h o s -> p h (o s)"),
                                             start=(c == 0), stop=(c == C - 1))
                    last.then_inc(scores_mm, 1)

                def attend(t):
                    pe.wait_ge(attn_ready, tile0 + (t + 1))
                    if t >= 1:
                        pe.wait_ge(attnT_sb, tile0 + t)
                    for m in range(M):
                        last = pe.transpose(attnT_bank[:, m, :], attn[:, t % 2, m * P:(m + 1) * P], ident[:])
                    last.then_inc(attnT_mm, 1)
                    pe.wait_ge(attnT_sb, tile0 + (t + 1))
                    if t >= 1:
                        pe.wait_ge(x1_ready, tile0 + t)
                    for m in range(M):
                        last = pe.matmul(out_bank[:, 0:D], attnT[:, m, :], VW[:, m, :], start=(m == 0), stop=(m == M - 1))
                    last.then_inc(out_mm, 1)

                def turn_x2(t):
                    pe.wait_ge(x2_ready, tile0 + (t + 1))
                    if t == 0:
                        pe.wait_ge(xnT_sb, tile0 + T)
                    else:
                        pe.wait_ge(x2T_sb, tile0 + t)
                    for c in range(C):
                        last = pe.transpose(turn_bank[:, c * P:(c + 1) * P], x2[:, t, c * P:(c + 1) * P], ident[:])
                    last.then_inc(x2T_mm, 1)

                pe.wait_ge(vTb_ready, b + 1)
                turn_xn(0)
                for k in range(4):
                    for odd in range(2):
                        last = pe.matmul(score_banks[k // 2][64 * odd:64 * odd + SC, 512 * (k % 2):512 * (k % 2) + 512], vT_b[:],
                                         Wo[:, 4 * k + odd:4 * k + odd + 3:2, :], start=True, stop=True)
                    last.then_inc(vw_mm, 1)
                for t in range(T + 2):
                    if t < T:
                        scores(t)
                    if t + 1 < T:
                        turn_xn(t + 1)
                    if 1 <= t <= T:
                        attend(t - 1)
                    if t >= 2:
                        turn_x2(t - 2)

        @block.scalar
        def _(act):
            act.wait_ge(kv_mm, 1)
            act.mul(kT[:], bank[0][0:DK, :], float(DK) ** -0.5).then_inc(kv_sb, 1)
            act.wait_ge(kv_mm, 2)
            act.copy(vT[:].rearrange("p b s -> p (b s)"), bank[1][0:DK, :]).then_inc(kv_sb, 1)
            act.wait_ge(kv_sb, 2)
            for n in range(0, C * H):
                c, h = divmod(n, H)
                act.wait_ge(g_mm, n + 1)
                act.copy(G[:, c, h, :, :].rearrange("p b s -> p (b s)"), bank[n % 2][:]).then_inc(g_sb, 1)

            with act.Fori(0, B) as b:
                tile0 = b * T

                def take_xnT(t):
                    act.wait_ge(xnT_mm, tile0 + (t + 1))
                    if t >= 2:
                        act.wait_ge(scores_mm, tile0 + (t - 1))
                    act.copy(xnT[:, t % 2, :, :].rearrange("p c n -> p (c n)"), turn_bank[:, 0:D]).then_inc(xnT_sb, 1)

                act.copy(vT_b[:], vT[:, bass.ds(b, 1), :].rearrange("p o s -> p (o s)")).then_inc(vTb_ready, 1)
                take_xnT(0)
                for k in range(4):
                    act.wait_ge(vw_mm, b * 4 + (k + 1))
                    act.copy(VW[:, 2 * k:2 * k + 2, :].rearrange("p m d -> p (m d)"),
                             score_banks[k // 2][:, 512 * (k % 2):512 * (k % 2) + 512]).then_inc(vw_sb, 1)
                for t in range(T + 2):
                    if t + 1 < T:
                        take_xnT(t + 1)
                    if t < T:
                        act.wait_ge(shifted, tile0 + (t + 1))
                        act.activation(attn[:, t % 2, :], attn[:, t % 2, :], ACT.Exp).then_inc(exped, 1)
                    if 1 <= t <= T:
                        act.wait_ge(attnT_mm, tile0 + t)
                        if t >= 2:
                            act.wait_ge(out_mm, tile0 + (t - 1))
                        act.copy(attnT[:].rearrange("p m n -> p (m n)"),
                                 attnT_bank[:].rearrange("p m n -> p (m n)")).then_inc(attnT_sb, 1)
                    if t >= 2:
                        act.wait_ge(x2T_mm, tile0 + (t - 1))
                        if t == 2:
                            act.wait_ge(x2T_stored, b * DMA + DMA)
                        act.copy(x2T[:, :, (t - 2) * P:(t - 1) * P],
                                 turn_bank[:, 0:D].rearrange("p (c n) -> p c n", c=C)).then_inc(x2T_sb, 1)

        @block.gpsimd
        def _(pool):
            pool.memset(minus_half[:], -0.5).then_inc(half_set, 1)
            pool.memset(seen[:], 1.0).then_inc(half_set, 1)
            pool.memset(hidden[:], 0.0).then_inc(half_set, 1)
            pool.wait_ge(half_set, 3)
            pool.affine_select(out=seen[:], in_=seen[:], compare_op=ALU.is_ge, fill=0.0, base=0,
                               pattern=[[-1, SC]], channel_multiplier=1).then_inc(mask_set, 1)
            pool.affine_select(out=hidden[:], in_=hidden[:], compare_op=ALU.is_ge, fill=NEG, base=0,
                               pattern=[[-1, SC]], channel_multiplier=1).then_inc(mask_set, 1)
            with pool.Fori(0, B) as b:
                tile0 = b * T
                norms = [0]

                def inverse_root():
                    norms[0] += 1
                    pool.wait_ge(var_ready, b * (2 * T) + norms[0])
                    pool.tensor_tensor(rstd[:], var_eps[:], minus_half[:], ALU.pow).then_inc(rstd_ready, 1)

                inverse_root()
                for t in range(T + 2):
                    if t + 1 < T:
                        inverse_root()
                    if t >= 2:
                        inverse_root()
                    if t >= T:
                        continue
                    pool.wait_ge(rz_ready, tile0 + (t + 1))
                    a = attn[:, t % 2, :].rearrange("p (h s) -> p h s", h=H)
                    pool.tensor_tensor(a, a, rz[:, t % 2, :].unsqueeze(2).to_broadcast([P, H, SC]),
                                       ALU.mult).then_inc(attn_ready, 1)

        STEPS = T * 6 + 2

        @block.vector
        def _(dve):
            dve.wait_ge(mask_set, 2)
            dve.memset(spare[:], 0.0)
            with dve.Fori(0, B) as b:
                tile0 = b * T
                steps, norms = [0], [0]

                def step(ins):
                    steps[0] += 1
                    ins.then_inc(dve_step, 1)
                    dve.wait_ge(dve_step, b * STEPS + steps[0])

                def normalise(dst, src, ready):
                    step(dve.bn_stats(stats[:], src))
                    dve.memset(spare[:], 0.0)
                    step(dve.bn_aggr(mv[:], stats[:]))
                    dve.tensor_scalar(var_eps[:], mv[:, 1:2], EPS, None, ALU.add).then_inc(var_ready, 1)
                    norms[0] += 1
                    dve.wait_ge(rstd_ready, b * (2 * T) + norms[0])
                    dve.tensor_scalar(dst, src, mv[:, 0:1], rstd[:], ALU.subtract, ALU.mult).then_inc(ready, 1)

                def norm_x(t):
                    dve.wait_ge(x_in[t], b * DMA + DMA)
                    if t >= 2:
                        dve.wait_ge(xnT_mm, tile0 + (t - 1))
                    normalise(xn[:, t % 2, :], xt[:, t, :], xn_ready)
                    dve.wait_ge(xn_ready, tile0 + (t + 1))

                def shift(t):
                    a = attn[:, t % 2, :].rearrange("p (h s) -> p h s", h=H)
                    dve.wait_ge(scores_mm, tile0 + (t + 1))
                    if t == 0:
                        step(dve.tensor_tensor(a, score_banks[0][:].rearrange("p (h s) -> p h s", h=H),
                                               seen[:].unsqueeze(1).to_broadcast([P, H, SC]), ALU.mult))
                        step(dve.tensor_tensor(a, a, hidden[:].unsqueeze(1).to_broadcast([P, H, SC]), ALU.add))
                        src = a
                    else:
                        src = score_banks[t % 2][:].rearrange("p (h s) -> p h s", h=H)
                        if t >= 2:
                            dve.wait_ge(attnT_mm, tile0 + (t - 1))
                    step(dve.tensor_reduce(mx[:], src, X, ALU.max))
                    dve.tensor_tensor(a, src, mx[:].unsqueeze(2).to_broadcast([P, H, SC]),
                                      ALU.subtract).then_inc(shifted, 1)

                def sums(t):
                    dve.wait_ge(exped, tile0 + (t + 1))
                    step(dve.tensor_reduce(total[:], attn[:, t % 2, :].rearrange("p (h s) -> p h s", h=H), X, ALU.add))
                    if t >= 2:
                        dve.wait_ge(attn_ready, tile0 + (t - 1))
                    dve.reciprocal(rz[:, t % 2, :], total[:]).then_inc(rz_ready, 1)
                    dve.wait_ge(rz_ready, tile0 + (t + 1))

                def finish(t):
                    dve.wait_ge(out_mm, tile0 + (t + 1))
                    if t == 0:
                        dve.wait_ge(tiles_stored, b * (T * 2 * DMA) + DMA)
                    dve.tensor_tensor(x1[:, t, :], out_bank[:, 0:D], xt[:, t, :], ALU.add).then_inc(x1_ready, 1)
                    dve.wait_ge(x1_ready, tile0 + (t + 1))
                    normalise(x2[:, t, :], x1[:, t, :], x2_ready)
                    dve.wait_ge(x2_ready, tile0 + (t + 1))

                norm_x(0)
                for t in range(T + 2):
                    if t + 1 < T:
                        norm_x(t + 1)
                    if t < T:
                        shift(t)
                    if t >= 2:
                        finish(t - 2)
                    if t < T:
                        sums(t)
                dve.wait_ge(x2T_sb, tile0 + T)
                dve.tensor_reduce(colsum[:, :, bass.ds(b, 1)], x2T[:], X, ALU.add).then_inc(colsum_done, 1)
                assert steps[0] == STEPS


def gate(nc, dram, index_dram, weight_dram, keep):
    with ExitStack() as ctx:
        def sb(name, shape, dt=F32):
            return ctx.enter_context(nc.sbuf_tensor(name, shape, dt))

        logits_ps = ctx.enter_context(nc.psum_tensor("logits_ps", [B, E], F32))
        colsum, index, weight = keep["colsum"], keep["index"], keep["weight"]
        gwT, gb = sb("gwT", [P, C, E]), sb("gb", [B, E])
        before, number = sb("before", [B, E, E]), sb("number", [B, TOPK, E])
        slot_no = sb("slot_no", [B, TOPK, E])
        logit, prob, mx, total = sb("logit", [B, E]), sb("prob", [B, E]), sb("g_mx", [B, 1]), sb("g_total", [B, 1])
        wins, ties = sb("wins", [B, E, E]), sb("ties", [B, E, E])
        rank, chosen = sb("rank", [B, E]), sb("chosen", [B, TOPK, E])
        idx_f, idx_i, wts = sb("idx_f", [B, TOPK]), sb("idx_i", [B, TOPK], I32), sb("wts", [B, TOPK])
        loaded = ctx.enter_context(nc.semaphore("g_loaded"))
        logits_mm = ctx.enter_context(nc.semaphore("g_logits_mm"))
        step_done = ctx.enter_context(nc.semaphore("g_step_done"))
        exped = ctx.enter_context(nc.semaphore("g_exped"))
        stored = ctx.enter_context(nc.semaphore("g_stored"))
        PRE_EXP, ALL = 4, 18
        block = ctx.enter_context(nc.Block())

        @block.sync
        def _(sp):
            sp.dma_start(gwT[:], dram["gate_wT"].rearrange("(c p) e -> p c e", p=P)).then_inc(loaded, DMA)
            for dst, src in ((gb, dram["gate_b"]), (before, dram["before"]), (number, dram["number"]),
                             (slot_no, dram["slot_no"])):
                sp.dma_start(dst[:], src).then_inc(loaded, DMA)
            sp.wait_ge(step_done, ALL)
            sp.dma_start(index_dram.rearrange("(b k) -> b k", k=TOPK), idx_i[:]).then_inc(stored, DMA)
            sp.dma_start(weight_dram.rearrange("(b k) -> b k", k=TOPK), wts[:]).then_inc(stored, DMA)
            sp.wait_ge(stored, 2 * DMA)
            sp.dma_start(index[:], index_dram.unsqueeze(0)).then_inc(loaded, DMA)
            sp.dma_start(weight[:], weight_dram.unsqueeze(0).to_broadcast([P, PAIRS])).then_inc(loaded, DMA)
            sp.wait_ge(loaded, 7 * DMA)

        @block.tensor
        def _(pe):
            pe.wait_ge(loaded, 5 * DMA)
            for c in range(C):
                last = pe.matmul(logits_ps[:], colsum[:, c, :], gwT[:, c, :], start=(c == 0), stop=(c == C - 1))
            last.then_inc(logits_mm, 1)

        @block.scalar
        def _(act):
            act.wait_ge(step_done, PRE_EXP)
            act.activation(prob[:], prob[:], ACT.Exp).then_inc(exped, 1)

        @block.vector
        def _(dve):
            n = [0]

            def step(ins):
                n[0] += 1
                ins.then_inc(step_done, 1)
                dve.wait_ge(step_done, n[0])

            def over_f(a):
                return a[:].unsqueeze(1).to_broadcast([B, E, E])

            def over_e(a):
                return a[:].unsqueeze(2).to_broadcast([B, E, E])

            def over_k(a):
                return a[:].unsqueeze(1).to_broadcast([B, TOPK, E])

            dve.wait_ge(loaded, 5 * DMA)
            dve.wait_ge(logits_mm, 1)
            step(dve.tensor_scalar(logit[:], logits_ps[:], 1.0 / S, None, ALU.mult))
            step(dve.tensor_tensor(logit[:], logit[:], gb[:], ALU.add))
            step(dve.tensor_reduce(mx[:], logit[:], X, ALU.max))
            step(dve.tensor_scalar(prob[:], logit[:], mx[:], None, ALU.subtract))
            assert n[0] == PRE_EXP
            step(dve.tensor_tensor(wins[:], over_f(logit), over_e(logit), ALU.is_gt))
            step(dve.tensor_tensor(ties[:], over_f(logit), over_e(logit), ALU.is_equal))
            step(dve.tensor_tensor(ties[:], ties[:], before[:], ALU.mult))
            step(dve.tensor_tensor(wins[:], wins[:], ties[:], ALU.add))
            step(dve.tensor_reduce(rank[:], wins[:], X, ALU.add))
            step(dve.tensor_tensor(chosen[:], over_k(rank), slot_no[:], ALU.is_equal))
            step(dve.tensor_tensor(number[:], chosen[:], number[:], ALU.mult))
            step(dve.tensor_reduce(idx_f[:], number[:], X, ALU.add))
            step(dve.tensor_copy(idx_i[:], idx_f[:]))
            dve.wait_ge(exped, 1)
            step(dve.tensor_reduce(total[:], prob[:], X, ALU.add))
            step(dve.reciprocal(total[:], total[:]))
            step(dve.tensor_scalar(prob[:], prob[:], total[:], None, ALU.mult))
            step(dve.tensor_tensor(chosen[:], chosen[:], over_k(prob), ALU.mult))
            step(dve.tensor_reduce(wts[:], chosen[:], X, ALU.add))
            assert n[0] == ALL


HG = 4
GROUPS = H // HG
PT = H // 2
KQ = 3 * HD
SHIFT_ROW = KQ
KC = S // P
STEPS = GROUPS * KC * 2
LEAD = 12
RING = 4
SLOTS = 28
QK, PROJ, TURN_Y, HID, FF, V = 0, 4, 8, 12, 20, 24
AT_QK, AT_PROJ, AT_TURN_Y, AT_HID, AT_FF = 2, 6, 9, 13, 21
AT_TURN = 5


def wait(eng, sem, value):
    if not (isinstance(value, int) and value <= 0):
        eng.wait_ge(sem, value)


def slot_count(i, n):
    before = 4 + 4 + (i - 1) * (SLOTS // 2)
    if isinstance(i, int) and i <= 0:
        n = n if n < PROJ else n - (V - PROJ)
        before = 0 if i < 0 else 4
    elif isinstance(i, int) and i == PAIRS:
        before, n = before - 4, n - PROJ
    elif isinstance(i, int) and i == PAIRS - 1:
        n = n - PROJ
    return before + (n // 2 + 1)


def stage_b(nc, dram, x2_dram, x2T_dram, qk_dram, z_dram, out, keep):
    with ExitStack() as ctx:
        def sb(name, shape, dt=F32):
            return ctx.enter_context(nc.sbuf_tensor(name, shape, dt))

        def ps(name, shape):
            return ctx.enter_context(nc.psum_tensor(name, shape, F32))

        def sem(name):
            return ctx.enter_context(nc.semaphore("b_" + name))

        st_banks, max_banks = ps("b_st", [P, 2, 512]), ps("b_max", [P, 2, 512])
        o_bank, turn_bank = ps("b_o", [P, 512]), ps("b_turn", [P, 512])
        shared = [ps("b_shared0", [P, 512]), ps("b_shared1", [P, 512])]

        ident, index, weight = keep["ident"], keep["index"], keep["weight"]
        w_qkv = sb("w_qkv", [P, C, 3 * D])
        w_out = sb("w_out", [P, GROUPS, D])
        w_1 = sb("w_1", [P, C, F])
        w_2 = sb("w_2", [P, M, D])
        b_qk, b_hid = sb("b_qk", [P, 4]), sb("b_hid", [P, M])
        b_v = sb("b_v", [P, D])
        rows = sb("rows", [P, 5, D])
        x2T = sb("x2T_b", [P, C, S])
        x2 = sb("x2_b", [P, T, D])
        acc = sb("acc", [P, T, D])
        qk32 = sb("qk32", [P, 2, S])
        qk_parts = sb("qk_parts", [P, 4, 2, S], F32R)
        q_stack = sb("q_stack", [P, PT, S], F32R)
        k_stack = sb("k_stack", [P, PT, S], F32R)
        v_aug = sb("v_aug", [P, KC, H, 2 * HD])
        neg_max = sb("neg_max", [P, GROUPS, T, HG])
        shift = sb("shift", [HG, S], F32R)
        prob = sb("prob_b", [P, RING, 2, S])
        o_raw = sb("o_raw", [P, GROUPS, S])
        z_turned = sb("z_turned", [P, H * S // P])
        rz_turned = sb("rz_turned", [P, H * S // P])
        rz = sb("rz_b", [P, GROUPS, S])
        o_norm = sb("o_norm", [P, GROUPS, S])
        r = sb("r", [P, 2, D])
        y1 = sb("y1", [P, T, D])
        y1_b = sb("y1_b", [P, T, D])
        y1T = sb("y1T", [P, C, S])
        hidden = sb("hidden_b", [P, M, S])
        stats, mv, rstd = sb("stats_b", [P, 6]), sb("mv_b", [P, 2]), sb("rstd_b", [P, 1])
        var_eps, minus_half = sb("var_eps_b", [P, 1]), sb("minus_half_b", [P, 1])
        spare, spare_pool = sb("spare_b", [P, 1]), sb("spare_pool", [P, 4])
        w_pair = sb("w_pair", [P, 1])

        consts_set = sem("consts_set")
        qkv_in, w_out_in, w_1_in, w_2_in = sem("qkv_in"), sem("w_out_in"), sem("w_1_in"), sem("w_2_in")
        x2_in, acc_in = sem("x2_in"), sem("acc_in")
        slot_mm = [sem("slot_mm0"), sem("slot_mm1")]
        slot_taken = [sem("slot_taken0"), sem("slot_taken1")]
        qk_high, qk_low = sem("qk_high"), sem("qk_low")
        qk_out = [sem(f"qk_out{u}") for u in range(4)]
        stacks_in = [sem("stacks_in_a"), sem("stacks_in_b")]
        max_mm, max_done = sem("max_mm"), sem("max_done")
        turn_mm, shift_sb, shift_in = sem("turn_mm"), sem("shift_sb"), sem("shift_in")
        st_mm, prob_ready, pv_mm, o_sb = sem("st_mm"), sem("prob_ready"), sem("pv_mm"), sem("o_sb")
        z_moved, z_inverted, rz_moved, rz_in, o_ready = (sem("z_moved"), sem("z_inverted"), sem("rz_moved"),
                                                         sem("rz_in"), sem("o_ready"))
        y1_ready, y1b_ready = sem("y1_ready"), sem("y1b_ready")
        acc_ready, stored = sem("acc_ready"), sem("stored")
        half_set, var_ready, rstd_ready = sem("half_set"), sem("var_ready"), sem("rstd_ready")
        dve_step = sem("dve_step")

        block = ctx.enter_context(nc.Block())

        def in_order(pair_iteration):
            def run(eng):
                pair_iteration(0, False, True)
                with eng.Fori(1, PAIRS - 1) as i:
                    pair_iteration(i, True, True)
                pair_iteration(PAIRS - 1, True, False)
            return run

        @block.sync
        def _(sp):
            def expert_of(i):
                return sp.value_load(index[:, bass.ds(i, 1)], min_val=0, max_val=E - 1)

            def whole(src, e):
                return src[bass.ds(e, 1)]

            def load_qkv(n, e):
                sp.dma_start(w_qkv[:], whole(dram["w_qkv"], e).rearrange("o p c n -> p (o c) n")).then_inc(qkv_in, DMA)
                sp.dma_start(b_qk[:], whole(dram["b_qk"], e).rearrange("o p n -> p (o n)")).then_inc(qkv_in, DMA)
                sp.dma_start(b_v[:], whole(dram["b_v"], e).to_broadcast([P, D])).then_inc(qkv_in, DMA)
                sp.dma_start(x2T[:], x2T_dram[bass.ds(n // TOPK, 1)].rearrange("o p c n -> p (o c) n")).then_inc(qkv_in, DMA)

            def load_w_out(e):
                for j in range(HG):
                    sp.dma_start(w_out[32 * j:32 * j + HD, :, :],
                                 whole(dram["w_out"], e)[:, j].rearrange("o p g n -> p (o g) n")).then_inc(w_out_in, DMA)
                sp.dma_start(w_out[HD:HD + 1, 0, :], whole(dram["b_out"], e)).then_inc(w_out_in, DMA)

            def load_w_1(e):
                sp.dma_start(w_1[:], whole(dram["w_1"], e).rearrange("o p c n -> p (o c) n")).then_inc(w_1_in, DMA)
                sp.dma_start(b_hid[:], whole(dram["b_hid"], e).rearrange("o p n -> p (o n)")).then_inc(w_1_in, DMA)

            def load_w_2(e):
                sp.dma_start(w_2[:], whole(dram["w_2"], e).rearrange("o p m n -> p (o m) n")).then_inc(w_2_in, DMA)
                sp.dma_start(rows[:], whole(dram["rows"], e).to_broadcast([P, 5, D])).then_inc(w_2_in, DMA)

            def load_rows_of(n):
                sp.dma_start(x2[:], x2_dram[bass.ds(n // TOPK, 1)].rearrange("o (t p) d -> p (o t) d", p=P)).then_inc(x2_in, DMA)
                sp.dma_start(acc[:], out[bass.ds(n // TOPK, 1)].rearrange("o (t p) d -> p (o t) d", p=P)).then_inc(acc_in, DMA)

            def parts_out(n):
                for u in range(4):
                    wait(sp, qk_high, n * 4 + (u + 1))
                    wait(sp, qk_low, n * 4 + (u + 1))
                    sp.dma_start(qk_dram[u], qk_parts[:, u, :, :].bitcast(F32)).then_inc(qk_out[u], DMA)

            def stacks_back(n, half):
                for u in range(4):
                    wait(sp, qk_out[u], n * DMA + DMA)
                    odd = u % 2
                    stack, order = (q_stack, (0, 0, 1)) if u < 2 else (k_stack, (0, 1, 0))
                    for block_no, part in enumerate(order):
                        row = 64 * odd + HD * block_no
                        sp.dma_start(stack[row:row + HD, 4 * half:4 * half + 4, :].bitcast(F32),
                                     qk_dram[u, 64 * half:64 * half + 64, part, :].rearrange(
                                         "(m p) n -> p m n", p=HD)).then_inc(stacks_in[half], DMA)

            def shift_rows(n, g):
                wait(sp, shift_sb, n * GROUPS + (g + 1))
                for j in range(HG):
                    row = 64 * (j % 2) + SHIFT_ROW
                    sp.dma_start(q_stack[row:row + 1, 2 * g + j // 2, :].bitcast(F32),
                                 shift[j:j + 1, :].bitcast(F32)).then_inc(shift_in, DMA)

            def store_sums(n):
                for t in range(T):
                    wait(sp, acc_ready, n * T + (t + 1))
                    sp.dma_start(out[bass.ds(n // TOPK, 1), t * P:(t + 1) * P, :].rearrange("o p d -> p (o d)"),
                                 acc[:, t, :]).then_inc(stored, DMA)

            sp.wait_ge(consts_set, 3)
            load_qkv(0, expert_of(0))
            parts_out(0)
            stacks_back(0, 0)
            stacks_back(0, 1)
            shift_rows(0, 0)

            def iteration(i, has_prev, has_next):
                e = expert_of(i)
                if has_next:
                    e_next = expert_of(i + 1)
                    for n in (0, 1):
                        wait(sp, slot_taken[n], slot_count(i - 1, V + 2 + n))
                    load_qkv(i + 1, e_next)
                if has_prev:
                    wait(sp, st_mm, i * STEPS)
                    stacks_back(i, 1)
                    if has_next:
                        parts_out(i + 1)
                else:
                    parts_out(i + 1)
                    load_w_out(e)
                    load_w_1(e)
                    load_w_2(e)
                    load_rows_of(0)
                shift_rows(i, 1)
                if has_prev:
                    wait(sp, slot_mm[1], slot_count(i, PROJ + 3))
                    load_w_out(e)
                shift_rows(i, 2)
                if has_next:
                    wait(sp, st_mm, i * STEPS + STEPS // 2)
                    stacks_back(i + 1, 0)
                if has_prev:
                    for n in (0, 1):
                        wait(sp, slot_taken[n], slot_count(i, HID + 6 + n))
                    load_w_1(e)
                shift_rows(i, 3)
                if has_prev:
                    store_sums(i - 1)
                    wait(sp, stored, i * (T * DMA))
                    load_rows_of(i)
                    load_w_2(e)
                if has_next:
                    shift_rows(i + 1, 0)

            in_order(iteration)(sp)
            store_sums(PAIRS - 1)
            sp.wait_ge(stored, PAIRS * T * DMA)

        @block.tensor
        def _(pe):
            def slot(i, n):
                wait(pe, slot_taken[n % 2], slot_count(i, n) - 1)
                return shared[n % 2]

            def stack_rows(h, extra):
                first = 64 * (h % 2)
                return slice(first, first + KQ + extra)

            def qk_tile(i, u):
                if u == 0:
                    wait(pe, qkv_in, i * (4 * DMA) + 8 * DMA)
                bank = slot(i, QK + u)
                for c in range(C):
                    last = pe.matmul(bank[:], w_qkv[:, c, u * P:(u + 1) * P], x2T[:, c, :], start=(c == 0), stop=(c == C - 1))
                last.then_inc(slot_mm[u % 2], 1)

            def v_tile(i, t):
                bank = slot(i, V + t)
                for c in range(C):
                    last = pe.matmul(bank[:, 0:D], x2T[:, c, t * P:(t + 1) * P], w_qkv[:, c, 2 * D:3 * D],
                                     start=(c == 0), stop=(c == C - 1))
                last.then_inc(slot_mm[t % 2], 1)

            def maxima(i, s):
                n, m = (i, s) if s < STEPS else (i + 1, s - STEPS)
                g, qc, j = m // 8, m % 8 // 2, 2 * (m % 2)
                if m % (STEPS // 2) == 0:
                    wait(pe, stacks_in[m // (STEPS // 2)], n * (12 * DMA) + 12 * DMA)
                wait(pe, max_done, n * STEPS + m)
                for k in range(2):
                    h = HG * g + j + k
                    last = pe.matmul(max_banks[:, k, :], q_stack[stack_rows(h, 0), h // 2, qc * P:(qc + 1) * P],
                                     k_stack[stack_rows(h, 0), h // 2, :], start=True, stop=True)
                last.then_inc(max_mm, 1)

            def turn_maxima(n, g):
                wait(pe, max_done, n * STEPS + 8 * (g + 1))
                wait(pe, shift_sb, n * GROUPS + g)
                for qc in range(T):
                    last = pe.transpose(turn_bank[0:HG, qc * P:(qc + 1) * P], neg_max[:, g, qc, :], ident[:])
                last.then_inc(turn_mm, 1)

            def scores(i, s):
                g, kc, half = s // 8, s % 8 // 2, s % 2
                if s % 8 == 0:
                    wait(pe, shift_in, i * (H * DMA) + (g + 1) * (HG * DMA))
                wait(pe, prob_ready, i * STEPS + s)
                for k in range(2):
                    h = HG * g + 2 * half + k
                    last = pe.matmul(st_banks[:, k, :], k_stack[stack_rows(h, 1), h // 2, kc * P:(kc + 1) * P],
                                     q_stack[stack_rows(h, 1), h // 2, :], start=True, stop=True)
                last.then_inc(st_mm, 1)

            def times_v(i, s):
                g, kc = s // 8, s % 8 // 2
                wait(pe, prob_ready, i * STEPS + (s + 1))
                if kc == 0:
                    wait(pe, o_sb, i * GROUPS + g)
                if s == 1:
                    for n in (0, 1):
                        wait(pe, slot_taken[n], slot_count(i - 1, V + 2 + n))
                for j in range(HG):
                    last = pe.matmul(o_bank[32 * j:32 * j + 32, :], v_aug[:, kc, HG * g + j, :],
                                     prob[:, (s - 1 + j // 2) % RING, j % 2, :], start=(kc == 0), stop=(kc == KC - 1))
                last.then_inc(pv_mm, 1)

            def project(i, t):
                if t == 0:
                    wait(pe, w_out_in, i * (5 * DMA))
                    wait(pe, o_ready, i * GROUPS)
                bank = slot(i, PROJ + t)
                for g in range(GROUPS):
                    last = pe.matmul(bank[:, 0:D], o_norm[:, g, t * P:(t + 1) * P], w_out[:, g, :],
                                     start=(g == 0), stop=(g == GROUPS - 1))
                last.then_inc(slot_mm[t % 2], 1)

            def turn_y(i, t):
                wait(pe, y1_ready, (i - 1) * T + (t + 1))
                bank = slot(i, TURN_Y + t)
                for c in range(C):
                    last = pe.transpose(bank[:, c * P:(c + 1) * P], y1[:, t, c * P:(c + 1) * P], ident[:])
                last.then_inc(slot_mm[t % 2], 1)

            def hidden_chunk(i, m):
                if m == 0:
                    wait(pe, w_1_in, i * (2 * DMA))
                    for n in (0, 1):
                        wait(pe, slot_taken[n], slot_count(i, TURN_Y + 2 + n))
                bank = slot(i, HID + m)
                for c in range(C):
                    last = pe.matmul(bank[:], w_1[:, c, m * P:(m + 1) * P], y1T[:, c, :], start=(c == 0), stop=(c == C - 1))
                last.then_inc(slot_mm[m % 2], 1)

            def feed_forward(i, t, half):
                if t == 0 and half == 0:
                    wait(pe, w_2_in, i * (2 * DMA))
                    for n in (0, 1):
                        wait(pe, slot_taken[n], slot_count(i, HID + 6 + n))
                bank = slot(i, FF + t) if half == 0 else shared[t % 2]
                for m in range(4 * half, 4 * half + 4):
                    last = pe.matmul(bank[:, 0:D], hidden[:, m, t * P:(t + 1) * P], w_2[:, m, :],
                                     start=(m == 0), stop=(m == M - 1))
                if half == 1:
                    last.then_inc(slot_mm[t % 2], 1)

            def of_last_pair(i, s):
                if AT_PROJ <= s < AT_PROJ + T:
                    project(i, s - AT_PROJ)
                if AT_TURN_Y <= s < AT_TURN_Y + T:
                    turn_y(i, s - AT_TURN_Y)
                if AT_HID <= s < AT_HID + M:
                    hidden_chunk(i, s - AT_HID)
                if AT_FF <= s < AT_FF + 2 * T:
                    feed_forward(i, (s - AT_FF) // 2, (s - AT_FF) % 2)

            pe.wait_ge(consts_set, 3)
            for u in range(4):
                qk_tile(-1, u)
            for t in range(T):
                v_tile(-1, t)
            for s in range(LEAD):
                maxima(0, s)
            turn_maxima(0, 0)

            def iteration(i, has_prev, has_next):
                for s in range(STEPS):
                    scores(i, s)
                    if has_next and AT_QK <= s < AT_QK + 4:
                        qk_tile(i, s - AT_QK)
                    if has_prev:
                        of_last_pair(i, s)
                    if has_next or LEAD + s < STEPS:
                        maxima(i, LEAD + s)
                    if s % 8 == AT_TURN:
                        if s // 8 + 1 < GROUPS:
                            turn_maxima(i, s // 8 + 1)
                        elif has_next:
                            turn_maxima(i + 1, 0)
                    if s % 2 == 1:
                        times_v(i, s)
                if has_next:
                    for t in range(T):
                        v_tile(i, t)

            in_order(iteration)(pe)
            for s in range(STEPS):
                of_last_pair(PAIRS, s)

        @block.scalar
        def _(act):
            def slot(i, n):
                wait(act, slot_mm[n % 2], slot_count(i, n))
                return shared[n % 2]

            def high_part(n, u):
                wait(act, slot_taken[u % 2], slot_count(n - 1, QK + u))
                act.copy(qk_parts[:, u, 0, :], qk32[:, u % 2, :]).then_inc(qk_high, 1)

            def take_shift(n, g):
                wait(act, turn_mm, n * GROUPS + (g + 1))
                wait(act, shift_in, n * (H * DMA) + g * (HG * DMA))
                act.copy(shift[:], turn_bank[0:HG, :]).then_inc(shift_sb, 1)

            def of_last_pair(i, s):
                if AT_TURN_Y <= s < AT_TURN_Y + T:
                    t = s - AT_TURN_Y
                    bank = slot(i, TURN_Y + t)
                    act.copy(y1T[:, :, t * P:(t + 1) * P],
                             bank[:, 0:D].rearrange("p (c n) -> p c n", c=C)).then_inc(slot_taken[t % 2], 1)
                if AT_HID <= s < AT_HID + M:
                    m = s - AT_HID
                    if m == 0:
                        wait(act, w_1_in, i * (2 * DMA))
                    bank = slot(i, HID + m)
                    act.activation(hidden[:, m, :], bank[:], ACT.Relu, bias=b_hid[:, m:m + 1]).then_inc(slot_taken[m % 2], 1)

            for u in range(4):
                high_part(0, u)
            take_shift(0, 0)

            def iteration(i, has_prev, has_next):
                for s in range(STEPS):
                    wait(act, st_mm, i * STEPS + (s + 1))
                    wait(act, pv_mm, i * (STEPS // 2) + (s - RING) // 2 + 1)
                    act.activation(prob[:, s % RING, :, :].rearrange("p n q -> p (n q)"),
                                   st_banks[:].rearrange("p n q -> p (n q)"), ACT.Exp).then_inc(prob_ready, 1)
                    if has_next and AT_QK <= s < AT_QK + 4:
                        high_part(i + 1, s - AT_QK)
                    if has_prev:
                        of_last_pair(i, s)
                    if s % 8 == AT_TURN:
                        if s // 8 + 1 < GROUPS:
                            take_shift(i, s // 8 + 1)
                        elif has_next:
                            take_shift(i + 1, 0)
                    if s % 8 == 7:
                        g = s // 8
                        wait(act, pv_mm, i * (STEPS // 2) + (s + 1) // 2)
                        if g == 0:
                            wait(act, o_ready, i * GROUPS)
                        act.copy(o_raw[:, g, :], o_bank[:]).then_inc(o_sb, 1)

            in_order(iteration)(act)
            for s in range(STEPS):
                of_last_pair(PAIRS, s)

        @block.gpsimd
        def _(pool):
            pool.memset(minus_half[:], -0.5).then_inc(half_set, 1)
            pool.wait_ge(half_set, 1)
            pool.memset(spare_pool[:], 0.0)

            def low_part(n, u):
                if u == 0:
                    for half in range(2):
                        wait(pool, stacks_in[half], n * (12 * DMA))
                wait(pool, qk_high, n * 4 + (u + 1))
                pool.tensor_tensor(qk_parts[:, u, 1, :], qk32[:, u % 2, :], qk_parts[:, u, 0, :].bitcast(F32),
                                   ALU.subtract).then_inc(qk_low, 1)

            def inverse_root(n, k):
                wait(pool, var_ready, n * (2 * T) + (k + 1))
                pool.tensor_tensor(rstd[:], var_eps[:], minus_half[:], ALU.pow).then_inc(rstd_ready, 1)

            def wait_then_dma(k, sem, value):
                wait(pool, sem, value)
                pool.tensor_tensor(spare_pool[:, k:k + 1], minus_half[:], minus_half[:], ALU.add)

            def spread_sums(n):
                wait_then_dma(0, o_sb, n * GROUPS + GROUPS)
                pool.dma_start(z_dram[0], o_raw[HD:P:2 * HD, :, :]).then_inc(z_moved, DMA)
                wait_then_dma(1, z_moved, n * (2 * DMA) + DMA)
                pool.dma_start(z_turned[:], z_dram[0].rearrange("j g (a n) -> (j g a) n", n=H * S // P)).then_inc(z_moved, DMA)
                wait_then_dma(2, z_inverted, n + 1)
                pool.dma_start(z_dram[1].rearrange("j g (a n) -> (j g a) n", n=H * S // P), rz_turned[:]).then_inc(rz_moved, DMA)
                wait_then_dma(3, rz_moved, n * DMA + DMA)
                for j in range(HG):
                    pool.dma_start(rz[32 * j:32 * j + 32, :, :],
                                   z_dram[1, j].unsqueeze(0).to_broadcast([32, GROUPS, S])).then_inc(rz_in, DMA)

            def norms(n):
                inverse_root(n, 0)
                for t in range(T):
                    if t + 1 < T:
                        inverse_root(n, t + 1)
                    wait(pool, y1_ready, n * T + (t + 1))
                    pool.tensor_tensor(y1_b[:, t, :], y1[:, t, :], rows[:, 0, :], ALU.add).then_inc(y1b_ready, 1)
                for t in range(T):
                    inverse_root(n, T + t)

            for u in range(4):
                low_part(0, u)

            def iteration(i, has_prev, has_next):
                if has_prev:
                    spread_sums(i - 1)
                if has_next:
                    for u in range(4):
                        low_part(i + 1, u)
                if has_prev:
                    norms(i - 1)

            in_order(iteration)(pool)
            spread_sums(PAIRS - 1)
            norms(PAIRS - 1)

        @block.vector
        def _(dve):
            dve.memset(w_out[:], 0.0).then_inc(consts_set, 1)
            dve.memset(k_stack[:].bitcast(F32), 1.0).then_inc(consts_set, 1)
            dve.memset(v_aug[:], 1.0).then_inc(consts_set, 1)
            dve.wait_ge(consts_set, 3)
            OWN = T * 4 + T * 5 + 1
            own = [0]

            def step(n, ins):
                own[0] += 1
                ins.then_inc(dve_step, 1)
                wait(dve, dve_step, n * OWN + own[0])

            def slot(i, n):
                wait(dve, slot_mm[n % 2], slot_count(i, n))
                return shared[n % 2]

            def full_qk(i, u):
                if u == 0:
                    wait(dve, qkv_in, i * (4 * DMA) + 8 * DMA)
                wait(dve, qk_low, (i + 1) * 4 + (u - 1))
                bank = slot(i, QK + u)
                dve.tensor_scalar(qk32[:, u % 2, :], bank[:], b_qk[:, u:u + 1], float(HD) ** -0.5 if u < 2 else 1.0,
                                  ALU.add, ALU.mult).then_inc(slot_taken[u % 2], 1)

            def take_v(i, t):
                if t == 0:
                    wait(dve, pv_mm, (i + 1) * (STEPS // 2))
                bank = slot(i, V + t)
                dve.tensor_tensor(v_aug[:, t, :, 0:HD], bank[:, 0:D].rearrange("p (h d) -> p h d", h=H),
                                  b_v[:].rearrange("p (h d) -> p h d", h=H), ALU.add).then_inc(slot_taken[t % 2], 1)

            def reduce_max(i, s):
                n, m = (i, s) if s < STEPS else (i + 1, s - STEPS)
                g, qc, j = m // 8, m % 8 // 2, 2 * (m % 2)
                wait(dve, max_mm, n * STEPS + (m + 1))
                dve.tensor_reduce(neg_max[:, g, qc, j:j + 2], max_banks[:], X, ALU.max, negate=True).then_inc(max_done, 1)

            def norm_begin(n, k, src):
                step(n, dve.bn_stats(stats[:], src))
                dve.memset(spare[:], 0.0)
                step(n, dve.bn_aggr(mv[:], stats[:]))
                dve.tensor_scalar(var_eps[:], mv[:, 1:2], EPS, None, ALU.add).then_inc(var_ready, 1)

            def norm_end(n, k, rt, w):
                wait(dve, rstd_ready, n * (2 * T) + (k + 1))
                step(n, dve.tensor_scalar(rt, rt, mv[:, 0:1], rstd[:], ALU.subtract, ALU.mult))
                step(n, dve.tensor_tensor(rt, rt, rows[:, w, :], ALU.mult))

            def first_begin(i, t):
                n, rt = i - 1, r[:, t % 2, :]
                if t == 0:
                    wait(dve, w_2_in, i * (2 * DMA))
                    wait(dve, x2_in, i * DMA)
                bank = slot(i, PROJ + t)
                dve.tensor_tensor(rt, bank[:, 0:D], x2[:, t, :], ALU.add).then_inc(slot_taken[t % 2], 1)
                wait(dve, slot_taken[t % 2], slot_count(i, PROJ + t))
                norm_begin(n, t, rt)

            def first_end(i, t):
                n, rt = i - 1, r[:, t % 2, :]
                norm_end(n, t, rt, 1)
                dve.tensor_tensor(y1[:, t, :], rt, rows[:, 2, :], ALU.add).then_inc(y1_ready, 1)

            def second_begin(i, t):
                n, rt = i - 1, r[:, t % 2, :]
                wait(dve, y1b_ready, n * T + (t + 1))
                bank = slot(i, FF + t)
                dve.tensor_tensor(rt, bank[:, 0:D], y1_b[:, t, :], ALU.add).then_inc(slot_taken[t % 2], 1)
                wait(dve, slot_taken[t % 2], slot_count(i, FF + t))
                norm_begin(n, T + t, rt)

            def second_end(i, t):
                n, rt = i - 1, r[:, t % 2, :]
                norm_end(n, T + t, rt, 3)
                step(n, dve.tensor_tensor(rt, rt, rows[:, 4, :], ALU.add))
                if t == 0:
                    wait(dve, acc_in, i * DMA)
                dve.scalar_tensor_tensor(out=acc[:, t, :], in0=rt, scalar=w_pair[:], in1=acc[:, t, :],
                                         op0=ALU.mult, op1=ALU.add).then_inc(acc_ready, 1)

            def of_last_pair(i, s):
                if s == AT_PROJ - 3:
                    own[0] = 0
                    step(i - 1, dve.tensor_copy(w_pair[:], weight[:, bass.ds(i - 1, 1)]))
                    wait(dve, z_moved, i * (2 * DMA))
                    dve.reciprocal(rz_turned[:], z_turned[:]).then_inc(z_inverted, 1)
                if s == AT_PROJ - 1:
                    wait(dve, rz_in, i * (HG * DMA))
                    for g in range(GROUPS):
                        dve.tensor_tensor(o_norm[:, g, :], o_raw[:, g, :], rz[:, g, :], ALU.mult).then_inc(o_ready, 1)
                if AT_PROJ < s <= AT_PROJ + T:
                    first_end(i, s - AT_PROJ - 1)
                if AT_PROJ <= s < AT_PROJ + T:
                    first_begin(i, s - AT_PROJ)
                if AT_FF + 1 <= s < AT_FF + 1 + 2 * T:
                    t, half = divmod(s - AT_FF - 1, 2)
                    (second_end if half else second_begin)(i, t)

            for u in range(4):
                full_qk(-1, u)
            for t in range(T):
                take_v(-1, t)
            for s in range(LEAD):
                reduce_max(0, s)

            def iteration(i, has_prev, has_next):
                for s in range(STEPS):
                    if has_next and AT_QK <= s < AT_QK + 4:
                        full_qk(i, s - AT_QK)
                    if has_next or LEAD + s < STEPS:
                        reduce_max(i, LEAD + s)
                    if has_prev:
                        of_last_pair(i, s)
                if has_next:
                    for t in range(T):
                        take_v(i, t)
                assert own[0] in (0, OWN)

            in_order(iteration)(dve)
            wait(dve, acc_ready, (PAIRS - 1) * T)
            for s in range(STEPS):
                of_last_pair(PAIRS, s)


def build(nc, dram, out):
    x2_dram = nc.dram_tensor("x2_scratch", (B, S, D), F32, kind="Internal").ap()
    x2T_dram = nc.dram_tensor("x2T_scratch", (B, P, C, S), F32, kind="Internal").ap()
    qk_dram = nc.dram_tensor("qk_scratch", (4, P, 2, S), F32, kind="Internal").ap()
    z_dram = nc.dram_tensor("z_scratch", (2, HG, GROUPS, S), F32, kind="Internal").ap()
    index_dram = nc.dram_tensor("index_scratch", (PAIRS,), I32, kind="Internal").ap()
    weight_dram = nc.dram_tensor("weight_scratch", (PAIRS,), F32, kind="Internal").ap()
    with ExitStack() as ctx:
        keep = {name: ctx.enter_context(nc.sbuf_tensor(name, shape, dt)) for name, shape, dt in (
            ("ident", [P, P], F32), ("colsum", [P, C, B], F32), ("index", [1, PAIRS], I32), ("weight", [P, PAIRS], F32))}
        stage_a(nc, dram, x2_dram, x2T_dram, out, keep)
        gate(nc, dram, index_dram, weight_dram, keep)
        stage_b(nc, dram, x2_dram, x2T_dram, qk_dram, z_dram, out, keep)


def kernel(**inputs):
    import numpy as np
    import concourse.bacc as bacc
    from concourse.bass_utils import run_bass_kernel_spmd

    def arr(name):
        return np.asarray(inputs[name])

    iw, ib = arr("L0_ffn_in_proj_w"), arr("L0_ffn_in_proj_b")

    def even_odd(a):
        return a.reshape(E, PT, 2, HD, -1).transpose(0, 2, 1, 3, 4).reshape(E, D, -1)

    qkv = np.concatenate([even_odd(iw[:, 0:D]), even_odd(iw[:, D:2 * D]), iw[:, 2 * D:]], axis=1)
    b_qk = np.concatenate([even_odd(ib[:, 0:D]), even_odd(ib[:, D:2 * D])], axis=1).reshape(E, 4, P)
    e = np.arange(E)
    arrays = {
        "x": arr("x"),
        "ctxT": arr("ctx_1024").reshape(B * SC, D).T,
        "Wk": arr("L0_xattn_W_k"), "Wv": arr("L0_xattn_W_v"),
        "WqT": arr("L0_xattn_W_q").reshape(D, H, DK).transpose(2, 1, 0),
        "Wo": arr("L0_xattn_W_o").reshape(H, DK, D).transpose(1, 0, 2),
        "gate_wT": arr("L0_ffn_gate_w").T,
        "gate_b": np.broadcast_to(arr("L0_ffn_gate_b"), (B, E)),
        "w_qkv": qkv.reshape(E, 3 * D, C, P).transpose(0, 3, 2, 1),
        "b_qk": b_qk.transpose(0, 2, 1),
        "b_hid": arr("L0_ffn_lin1_b").reshape(E, M, P).transpose(0, 2, 1),
        "b_v": ib[:, 2 * D:],
        "w_out": arr("L0_ffn_out_proj_w").reshape(E, D, GROUPS, HG, HD).transpose(0, 3, 4, 2, 1),
        "b_out": arr("L0_ffn_out_proj_b"),
        "w_1": arr("L0_ffn_lin1_w").reshape(E, F, C, P).transpose(0, 3, 2, 1),
        "w_2": arr("L0_ffn_lin2_w").reshape(E, D, M, P).transpose(0, 3, 2, 1),
        "rows": np.stack([arr("L0_ffn_" + n) for n in ("lin2_b", "ln1_w", "ln1_b", "ln2_w", "ln2_b")], axis=1),
        "ident": np.eye(P, dtype=np.float32),
        "before": np.broadcast_to(e[None, :] < e[:, None], (B, E, E)).astype(np.float32),
        "number": np.broadcast_to(e, (B, TOPK, E)).astype(np.float32),
        "slot_no": np.broadcast_to(np.arange(TOPK)[:, None], (B, TOPK, E)).astype(np.float32),
    }
    nc = bacc.Bacc("TRN2", target_bir_lowering=False, num_devices=1)
    arrays = {f"in_{n}": np.ascontiguousarray(a) for n, a in arrays.items()}
    dram = {n[3:]: nc.dram_tensor(n, a.shape, mybir.dt.from_np(a.dtype), kind="ExternalInput").ap()
            for n, a in arrays.items()}
    out = nc.dram_tensor("out", (B, S, D), F32, kind="ExternalOutput").ap()
    build(nc, dram, out)
    r = run_bass_kernel_spmd(nc, [arrays], core_ids=[0])
    return r.results[0]["out"]
```

```python
from contextlib import ExitStack

import concourse.bass as bass
from concourse import mybir

ALU = mybir.AluOpType
ACT = mybir.ActivationFunctionType
X = mybir.AxisListType.X
F32 = mybir.dt.float32
F32R = mybir.dt.float32r
I32 = mybir.dt.int32

P = 128
B, S, D = 8, 512, 256
T = S // P
C = D // P
SC = 64
H = 16
DK = 64
HD = D // H
E = 4
TOPK = 2
PAIRS = B * TOPK
F = 1024
M = F // P
EPS = 1e-5
NEG = -1e9
POOL_HEADS = 6
DMA = 16


def due(value):
    return not (isinstance(value, int) and value <= 0)


def stage_a(nc, dram, x2_dram, x2T_dram, out, keep):
    with ExitStack() as ctx:
        def sb(name, shape, dt=F32):
            return ctx.enter_context(nc.sbuf_tensor(name, shape, dt))

        def sem(name):
            return ctx.enter_context(nc.semaphore(name))

        bank = [ctx.enter_context(nc.psum_tensor(f"a_bank{n}", [P, 512], F32)) for n in range(6, 8)]
        score_banks = [ctx.enter_context(nc.psum_tensor(f"a_scores{n}", [P, H * SC], F32)) for n in range(2)]
        attnT_bank = ctx.enter_context(nc.psum_tensor("a_attnT", [P, M, P], F32))
        turn_bank, out_bank = bank

        ident, colsum = keep["ident"], keep["colsum"]
        ctxT = sb("ctxT", [P, C, B * SC])
        Wk = sb("Wk", [P, C, DK])
        Wv = sb("Wv", [P, C, DK])
        WqT = sb("WqT", [DK, H, D])
        Wo = sb("Wo", [DK, H, D])
        kT = sb("kT", [DK, B * SC])
        vT = sb("vT", [DK, B, SC])
        vT_b = sb("vT_b", [DK, SC])
        G = sb("G", [P, C, H, B, SC])
        VW = sb("VW", [P, M, D])
        xt = sb("xt", [P, T, D])
        xn = sb("xn", [P, 2, D])
        xnT = sb("xnT", [P, 2, C, P])
        attn = sb("attn", [P, 2, H * SC])
        attnT = sb("attnT", [P, M, P])
        x1 = sb("x1", [P, T, D])
        x2 = sb("x2", [P, T, D])
        x2T = sb("x2T_a", [P, C, S])
        stats = [sb("stats_x", [P, 6]), sb("stats_1", [P, 6])]
        mv = [sb("mv_x", [P, 2]), sb("mv_1", [P, 2])]
        var_eps = [sb("var_eps_x", [P, 1]), sb("var_eps_1", [P, 1])]
        rstd = [sb("rstd_x", [P, 1]), sb("rstd_1", [P, 1])]
        spare = sb("spare_a", [P, 1])
        seen, hidden = sb("seen", [P, SC]), sb("hidden_a", [P, SC])
        minus_half = sb("minus_half_a", [P, 1])
        mx = sb("mx", [P, H])
        total = sb("total", [P, H])
        rz = sb("rz", [P, 2, H])

        consts_in = sem("a_consts_in")
        x_in = [sem(f"a_x_in{t}") for t in range(T)]
        kv_mm, kv_sb = sem("a_kv_mm"), sem("a_kv_sb")
        g_mm, g_sb = sem("a_g_mm"), sem("a_g_sb")
        vTb_ready = sem("a_vTb_ready")
        vw_mm, vw_sb = sem("a_vw_mm"), sem("a_vw_sb")
        xn_ready, xnT_mm, xnT_sb = sem("a_xn_ready"), sem("a_xnT_mm"), sem("a_xnT_sb")
        scores_mm = sem("a_scores_mm")
        mask_set = sem("a_mask_set")
        shifted, exped = sem("a_shifted"), sem("a_exped")
        rz_ready = sem("a_rz_ready")
        attn_ready, attn_ready_dve = sem("a_attn_ready"), sem("a_attn_ready_dve")
        attnT_mm, attnT_sb = sem("a_attnT_mm"), sem("a_attnT_sb")
        out_mm, x1_ready, x2_ready = sem("a_out_mm"), sem("a_x1_ready"), sem("a_x2_ready")
        x2T_mm, x2T_sb = sem("a_x2T_mm"), sem("a_x2T_sb")
        colsum_done = sem("a_colsum_done")
        tile_stored = [sem(f"a_tile_stored{t}") for t in range(T)]
        x2T_stored, half_set = sem("a_x2T_stored"), sem("a_half_set")
        var_ready = [sem("a_var_x_ready"), sem("a_var_1_ready")]
        rstd_ready = [sem("a_rstd_x_ready"), sem("a_rstd_1_ready")]
        dve_step = sem("a_dve_step")

        block = ctx.enter_context(nc.Block())

        def in_order(eng, steps):
            steps(0, True, False)
            with eng.Fori(1, B - 1) as b:
                steps(b, False, False)
            steps(B - 1, False, True)

        def behind(first, t, n):
            return t >= n or not first

        @block.sync
        def _(sp):
            for t in range(T):
                sp.sem_inc(tile_stored[t], DMA)
            for t in range(2):
                sp.dma_start(xt[:, t, :], dram["x"][0, t * P:(t + 1) * P, :]).then_inc(x_in[t], DMA)
            for dst, src in ((ctxT, dram["ctxT"].rearrange("(c p) n -> p c n", p=P)),
                             (Wk, dram["Wk"].rearrange("(c p) n -> p c n", p=P)),
                             (Wv, dram["Wv"].rearrange("(c p) n -> p c n", p=P)),
                             (WqT, dram["WqT"]), (ident, dram["ident"]), (Wo, dram["Wo"])):
                sp.dma_start(dst[:], src).then_inc(consts_in, DMA)
            for t in range(2, T):
                sp.dma_start(xt[:, t, :], dram["x"][0, t * P:(t + 1) * P, :]).then_inc(x_in[t], DMA)

            def store_tile(bm, t, n, prefetch):
                rows = slice(t * P, (t + 1) * P)
                sp.wait_ge(x2_ready, n + 1)
                if prefetch:
                    sp.dma_start(xt[:, t, :], dram["x"][bass.ds(bm + 1, 1), rows, :].rearrange(
                        "o p d -> p (o d)")).then_inc(x_in[t], DMA)
                sp.dma_start(out[bass.ds(bm, 1), rows, :].rearrange("o p d -> p (o d)"),
                             x1[:, t, :]).then_inc(tile_stored[t], DMA)
                sp.dma_start(x2_dram[bass.ds(bm, 1), rows, :].rearrange("o p d -> p (o d)"),
                             x2[:, t, :]).then_inc(tile_stored[t], DMA)

            def store_x2T(bm):
                sp.wait_ge(x2T_sb, bm * T + T)
                for c in reversed(range(C)):
                    sp.dma_start(x2T_dram[bass.ds(bm, 1), :, c, :].rearrange("o p n -> p (o n)"),
                                 x2T[:, c, :]).then_inc(x2T_stored, DMA)

            def steps(b, first, last):
                for t in range(T):
                    if behind(first, t, 2):
                        store_tile(b if t >= 2 else b - 1, (t - 2) % T, b * T + t - 2, not (last and t >= 2))
                    if t == 1 and not first:
                        store_x2T(b - 1)

            in_order(sp, steps)
            for t in (2, 3):
                store_tile(B - 1, t, (B - 1) * T + t, False)
            store_x2T(B - 1)
            for t in range(T):
                sp.wait_ge(tile_stored[t], B * 2 * DMA + DMA)
            sp.wait_ge(x2T_stored, B * C * DMA)

        @block.tensor
        def _(pe):
            pe.wait_ge(consts_in, 6 * DMA)
            for n, w in enumerate((Wk, Wv)):
                for c in range(C):
                    last = pe.matmul(bank[n][0:DK, :], w[:, c, :], ctxT[:, c, :], start=(c == 0), stop=(c == C - 1))
                last.then_inc(kv_mm, 1)
            pe.wait_ge(kv_sb, 2)
            for n in range(C * H):
                c, h = divmod(n, H)
                if n >= 2:
                    pe.wait_ge(g_sb, n - 1)
                pe.matmul(bank[n % 2][:], WqT[:, h, c * P:(c + 1) * P], kT[:], start=True,
                          stop=True).then_inc(g_mm, 1)
            pe.wait_ge(g_sb, C * H)

            def turn_xn(t, n):
                pe.wait_ge(xn_ready, n + 1)
                if due(n - 3):
                    pe.wait_ge(x2T_sb, n - 3)
                for c in range(C):
                    last = pe.transpose(turn_bank[:, c * P:(c + 1) * P], xn[:, t % 2, c * P:(c + 1) * P], ident[:])
                last.then_inc(xnT_mm, 1)

            def scores(b, t, n, half):
                if half == 0:
                    pe.wait_ge(xnT_sb, n + 1)
                    if t == 1:
                        pe.wait_ge(vw_sb, b * 4 + 4)
                    else:
                        if due(n - 1):
                            pe.wait_ge(shifted, n - 1)
                for c in range(C):
                    last = pe.matmul(score_banks[t % 2][:, half * 512:(half + 1) * 512], xnT[:, t % 2, c, :],
                                     G[:, c, half * 8:half * 8 + 8, bass.ds(b, 1), :].rearrange("p h o s -> p h (o s)"),
                                     start=(c == 0), stop=(c == C - 1))
                if half == 1:
                    last.then_inc(scores_mm, 1)

            def turn_attn(t, n):
                pe.wait_ge(attn_ready, n + 1)
                pe.wait_ge(attn_ready_dve, n + 1)
                if due(n):
                    pe.wait_ge(attnT_sb, n)
                for m in range(M):
                    last = pe.transpose(attnT_bank[:, m, :], attn[:, t % 2, m * P:(m + 1) * P], ident[:])
                last.then_inc(attnT_mm, 1)

            def attend(n):
                pe.wait_ge(attnT_sb, n + 1)
                if due(n):
                    pe.wait_ge(x1_ready, n)
                for m in range(M):
                    last = pe.matmul(out_bank[:, 0:D], attnT[:, m, :], VW[:, m, :], start=(m == 0), stop=(m == M - 1))
                last.then_inc(out_mm, 1)

            def values(b):
                for k in range(4):
                    for odd in range(2):
                        dst = score_banks[1][64 * odd:64 * odd + SC, 512 * k:512 * k + 512] if k < 2 else \
                            attnT_bank[64 * odd:64 * odd + SC, 4 * k - 8:4 * k - 4, :].rearrange("p m n -> p (m n)")
                        last = pe.matmul(dst, vT_b[:], Wo[:, 4 * k + odd:4 * k + odd + 3:2, :], start=True, stop=True)
                    last.then_inc(vw_mm, 1)

            def turn_x2(t, n):
                pe.wait_ge(x2_ready, n + 1)
                pe.wait_ge(xnT_sb, min(n + 4, B * T) if isinstance(n, int) else n + 4)
                if due(n):
                    pe.wait_ge(x2T_sb, n)
                for c in range(C):
                    last = pe.transpose(turn_bank[:, D + c * P:D + (c + 1) * P], x2[:, t, c * P:(c + 1) * P], ident[:])
                last.then_inc(x2T_mm, 1)

            def steps(b, first, last):
                for t in range(T):
                    n = b * T + t
                    scores(b, t, n, 0)
                    if behind(first, t, 1):
                        turn_attn((t - 1) % T, n - 1)
                    scores(b, t, n, 1)
                    if not (last and t == T - 1):
                        turn_xn((t + 1) % T, n + 1)
                    if t == 0:
                        pe.wait_ge(vTb_ready, b + 1)
                    if behind(first, t, 1):
                        attend(n - 1)
                    if t == 0:
                        values(b)
                    if behind(first, t, 2):
                        turn_x2((t - 2) % T, n - 2)

            turn_xn(0, 0)
            in_order(pe, steps)
            turn_attn(T - 1, B * T - 1)
            attend(B * T - 1)
            turn_x2(T - 2, B * T - 2)
            turn_x2(T - 1, B * T - 1)

        @block.scalar
        def _(act):
            act.wait_ge(kv_mm, 1)
            act.mul(kT[:], bank[0][0:DK, :], float(DK) ** -0.5).then_inc(kv_sb, 1)
            act.wait_ge(kv_mm, 2)
            act.copy(vT[:].rearrange("p b s -> p (b s)"), bank[1][0:DK, :]).then_inc(kv_sb, 1)
            act.wait_ge(kv_sb, 2)
            for n in range(0, C * H):
                c, h = divmod(n, H)
                act.wait_ge(g_mm, n + 1)
                act.copy(G[:, c, h, :, :].rearrange("p b s -> p (b s)"), bank[n % 2][:]).then_inc(g_sb, 1)

            def take_xnT(t, n):
                act.wait_ge(xnT_mm, n + 1)
                if due(n - 1):
                    act.wait_ge(scores_mm, n - 1)
                act.copy(xnT[:, t % 2, :, :].rearrange("p c n -> p (c n)"), turn_bank[:, 0:D]).then_inc(xnT_sb, 1)

            def take_attnT(n):
                act.wait_ge(attnT_mm, n + 1)
                act.copy(attnT[:].rearrange("p m n -> p (m n)"),
                         attnT_bank[:].rearrange("p m n -> p (m n)")).then_inc(attnT_sb, 1)

            def take_x2T(t, n, bm):
                act.wait_ge(x2T_mm, n + 1)
                if t == 0:
                    if due(bm * (C * DMA)):
                        act.wait_ge(x2T_stored, bm * (C * DMA))
                    if due(bm):
                        act.wait_ge(colsum_done, bm)
                act.copy(x2T[:, :, t * P:(t + 1) * P],
                         turn_bank[:, D:2 * D].rearrange("p (c n) -> p c n", c=C)).then_inc(x2T_sb, 1)

            def steps(b, first, last):
                for t in range(T):
                    n = b * T + t
                    if t == 0:
                        act.copy(vT_b[:], vT[:, bass.ds(b, 1), :].rearrange("p o s -> p (o s)")).then_inc(vTb_ready, 1)
                    if behind(first, t, 1):
                        take_attnT(n - 1)
                    if not (last and t == T - 1):
                        take_xnT((t + 1) % T, n + 1)
                    act.wait_ge(shifted, n + 1)
                    act.activation(attn[:, t % 2, :], attn[:, t % 2, :], ACT.Exp).then_inc(exped, 1)
                    if t == 0:
                        if due(n):
                            act.wait_ge(out_mm, n)
                        for k in range(4):
                            act.wait_ge(vw_mm, b * 4 + (k + 1))
                            src = score_banks[1][:, 512 * k:512 * k + 512] if k < 2 else \
                                attnT_bank[:, 4 * k - 8:4 * k - 4, :].rearrange("p m n -> p (m n)")
                            act.copy(VW[:, 2 * k:2 * k + 2, :].rearrange("p m d -> p (m d)"), src).then_inc(vw_sb, 1)
                    if behind(first, t, 2):
                        take_x2T((t - 2) % T, n - 2, b)

            take_xnT(0, 0)
            in_order(act, steps)
            take_attnT(B * T - 1)
            take_x2T(T - 2, B * T - 2, B - 1)
            take_x2T(T - 1, B * T - 1, B - 1)

        @block.gpsimd
        def _(pool):
            pool.memset(minus_half[:], -0.5).then_inc(half_set, 1)
            pool.memset(seen[:], 1.0).then_inc(half_set, 1)
            pool.memset(hidden[:], 0.0).then_inc(half_set, 1)
            pool.wait_ge(half_set, 3)
            pool.affine_select(out=seen[:], in_=seen[:], compare_op=ALU.is_ge, fill=0.0, base=0,
                               pattern=[[-1, SC]], channel_multiplier=1).then_inc(mask_set, 1)
            pool.affine_select(out=hidden[:], in_=hidden[:], compare_op=ALU.is_ge, fill=NEG, base=0,
                               pattern=[[-1, SC]], channel_multiplier=1).then_inc(mask_set, 1)

            def inverse_root(k, n):
                pool.wait_ge(var_ready[k], n + 1)
                pool.tensor_tensor(rstd[k][:], var_eps[k][:], minus_half[:], ALU.pow).then_inc(rstd_ready[k], 1)

            def steps(b, first, last):
                for t in range(T):
                    n = b * T + t
                    if not (last and t == T - 1):
                        inverse_root(0, n + 1)
                    if behind(first, t, 2):
                        inverse_root(1, n - 2)
                    pool.wait_ge(rz_ready, n + 1)
                    a = attn[:, t % 2, :].rearrange("p (h s) -> p h s", h=H)[:, 0:POOL_HEADS, :]
                    pool.tensor_tensor(a, a, rz[:, t % 2, 0:POOL_HEADS].unsqueeze(2).to_broadcast([P, POOL_HEADS, SC]),
                                       ALU.mult).then_inc(attn_ready, 1)

            inverse_root(0, 0)
            in_order(pool, steps)
            inverse_root(1, B * T - 2)
            inverse_root(1, B * T - 1)

        @block.vector
        def _(dve):
            dve.wait_ge(mask_set, 2)
            dve.memset(spare[:], 0.0)
            count, start = [0], [0]

            def step(ins):
                count[0] += 1
                ins.then_inc(dve_step, 1)
                dve.wait_ge(dve_step, start[0] + count[0])

            def norm_begin(k, src):
                step(dve.bn_stats(stats[k][:], src))
                dve.memset(spare[:], 0.0)
                step(dve.bn_aggr(mv[k][:], stats[k][:]))
                dve.tensor_scalar(var_eps[k][:], mv[k][:, 1:2], EPS, None, ALU.add).then_inc(var_ready[k], 1)

            def norm_end(k, n, dst, src, ready):
                dve.wait_ge(rstd_ready[k], n + 1)
                dve.tensor_scalar(dst, src, mv[k][:, 0:1], rstd[k][:], ALU.subtract, ALU.mult).then_inc(ready, 1)
                dve.wait_ge(ready, n + 1)

            def norm_x_begin(t, bn):
                dve.wait_ge(x_in[t], bn * DMA + DMA)
                norm_begin(0, xt[:, t, :])

            def norm_x_end(t, n):
                if due(n - 1):
                    dve.wait_ge(xnT_mm, n - 1)
                norm_end(0, n, xn[:, t % 2, :], xt[:, t, :], xn_ready)

            def largest(t, n):
                a = attn[:, t % 2, :].rearrange("p (h s) -> p h s", h=H)
                dve.wait_ge(scores_mm, n + 1)
                if due(n - 1):
                    dve.wait_ge(attnT_mm, n - 1)
                src = score_banks[t % 2][:].rearrange("p (h s) -> p h s", h=H)
                if t == 0:
                    step(dve.tensor_tensor(a, src, seen[:].unsqueeze(1).to_broadcast([P, H, SC]), ALU.mult))
                    step(dve.tensor_tensor(a, a, hidden[:].unsqueeze(1).to_broadcast([P, H, SC]), ALU.add))
                    src = a
                step(dve.tensor_reduce(mx[:], src, X, ALU.max))
                return a, src

            def shift(a, src):
                dve.tensor_tensor(a, src, mx[:].unsqueeze(2).to_broadcast([P, H, SC]), ALU.subtract).then_inc(shifted, 1)

            def sums(t, n):
                dve.wait_ge(exped, n + 1)
                step(dve.tensor_reduce(total[:], attn[:, t % 2, :].rearrange("p (h s) -> p h s", h=H), X, ALU.add))
                if due(n - 1):
                    dve.wait_ge(attn_ready, n - 1)
                if due(n - 1):
                    dve.wait_ge(attn_ready_dve, n - 1)
                dve.reciprocal(rz[:, t % 2, :], total[:]).then_inc(rz_ready, 1)
                dve.wait_ge(rz_ready, n + 1)
                a = attn[:, t % 2, :].rearrange("p (h s) -> p h s", h=H)[:, POOL_HEADS:, :]
                dve.tensor_tensor(a, a, rz[:, t % 2, POOL_HEADS:].unsqueeze(2).to_broadcast([P, H - POOL_HEADS, SC]),
                                  ALU.mult).then_inc(attn_ready_dve, 1)

            def finish_begin(t, n, bm):
                dve.wait_ge(out_mm, n + 1)
                dve.wait_ge(tile_stored[t], bm * (2 * DMA) + DMA)
                dve.tensor_tensor(x1[:, t, :], out_bank[:, 0:D], xt[:, t, :], ALU.add).then_inc(x1_ready, 1)
                dve.wait_ge(x1_ready, n + 1)
                norm_begin(1, x1[:, t, :])

            def finish_end(t, n):
                norm_end(1, n, x2[:, t, :], x1[:, t, :], x2_ready)

            def column_sums(bm):
                dve.wait_ge(x2T_sb, bm * T + T)
                dve.tensor_reduce(colsum[:, :, bass.ds(bm, 1)], x2T[:], X, ALU.add).then_inc(colsum_done, 1)

            def steps(b, first, last):
                if not (first or last):
                    outside = start[0] + count[0]
                    start[0], count[0] = outside + (b - 1) * LOOP_STEPS, 0
                for t in range(T):
                    n = b * T + t
                    ahead = not (last and t == T - 1)
                    if ahead:
                        norm_x_begin((t + 1) % T, b if t + 1 < T else b + 1)
                    if behind(first, t, 2):
                        finish_begin((t - 2) % T, n - 2, b if t >= 2 else b - 1)
                    if ahead:
                        norm_x_end((t + 1) % T, n + 1)
                    a, src = largest(t, n)
                    shift(a, src)
                    if behind(first, t, 2):
                        finish_end((t - 2) % T, n - 2)
                    sums(t, n)
                    if t == 1 and not first:
                        column_sums(b - 1)
                if not (first or last):
                    assert count[0] == LOOP_STEPS
                    start[0], count[0] = outside + (B - 2) * LOOP_STEPS, 0

            LOOP_STEPS = T * 6 + 2
            norm_x_begin(0, 0)
            norm_x_end(0, 0)
            in_order(dve, steps)
            for t in (T - 2, T - 1):
                finish_begin(t, (B - 1) * T + t, B - 1)
                finish_end(t, (B - 1) * T + t)
            column_sums(B - 1)


def gate(nc, dram, index_dram, weight_dram, keep):
    with ExitStack() as ctx:
        def sb(name, shape, dt=F32):
            return ctx.enter_context(nc.sbuf_tensor(name, shape, dt))

        logits_ps = ctx.enter_context(nc.psum_tensor("logits_ps", [B, E], F32))
        colsum, index, weight = keep["colsum"], keep["index"], keep["weight"]
        gwT, gb = sb("gwT", [P, C, E]), sb("gb", [B, E])
        before, number = sb("before", [B, E, E]), sb("number", [B, TOPK, E])
        slot_no = sb("slot_no", [B, TOPK, E])
        logit, prob, mx, total = sb("logit", [B, E]), sb("prob", [B, E]), sb("g_mx", [B, 1]), sb("g_total", [B, 1])
        wins, ties = sb("wins", [B, E, E]), sb("ties", [B, E, E])
        rank, chosen = sb("rank", [B, E]), sb("chosen", [B, TOPK, E])
        idx_f, idx_i, wts = sb("idx_f", [B, TOPK]), sb("idx_i", [B, TOPK], I32), sb("wts", [B, TOPK])
        loaded = ctx.enter_context(nc.semaphore("g_loaded"))
        logits_mm = ctx.enter_context(nc.semaphore("g_logits_mm"))
        step_done = ctx.enter_context(nc.semaphore("g_step_done"))
        exped = ctx.enter_context(nc.semaphore("g_exped"))
        stored = ctx.enter_context(nc.semaphore("g_stored"))
        PRE_EXP, ALL = 4, 18
        block = ctx.enter_context(nc.Block())

        @block.sync
        def _(sp):
            sp.dma_start(gwT[:], dram["gate_wT"].rearrange("(c p) e -> p c e", p=P)).then_inc(loaded, DMA)
            for dst, src in ((gb, dram["gate_b"]), (before, dram["before"]), (number, dram["number"]),
                             (slot_no, dram["slot_no"])):
                sp.dma_start(dst[:], src).then_inc(loaded, DMA)
            sp.wait_ge(step_done, ALL)
            sp.dma_start(index_dram.rearrange("(b k) -> b k", k=TOPK), idx_i[:]).then_inc(stored, DMA)
            sp.dma_start(weight_dram.rearrange("(b k) -> b k", k=TOPK), wts[:]).then_inc(stored, DMA)
            sp.wait_ge(stored, 2 * DMA)
            sp.dma_start(index[:], index_dram.unsqueeze(0)).then_inc(loaded, DMA)
            sp.dma_start(weight[:], weight_dram.unsqueeze(0).to_broadcast([P, PAIRS])).then_inc(loaded, DMA)
            sp.wait_ge(loaded, 7 * DMA)

        @block.tensor
        def _(pe):
            pe.wait_ge(loaded, 5 * DMA)
            for c in range(C):
                last = pe.matmul(logits_ps[:], colsum[:, c, :], gwT[:, c, :], start=(c == 0), stop=(c == C - 1))
            last.then_inc(logits_mm, 1)

        @block.scalar
        def _(act):
            act.wait_ge(step_done, PRE_EXP)
            act.activation(prob[:], prob[:], ACT.Exp).then_inc(exped, 1)

        @block.vector
        def _(dve):
            n = [0]

            def step(ins):
                n[0] += 1
                ins.then_inc(step_done, 1)
                dve.wait_ge(step_done, n[0])

            def over_f(a):
                return a[:].unsqueeze(1).to_broadcast([B, E, E])

            def over_e(a):
                return a[:].unsqueeze(2).to_broadcast([B, E, E])

            def over_k(a):
                return a[:].unsqueeze(1).to_broadcast([B, TOPK, E])

            dve.wait_ge(loaded, 5 * DMA)
            dve.wait_ge(logits_mm, 1)
            step(dve.tensor_scalar(logit[:], logits_ps[:], 1.0 / S, None, ALU.mult))
            step(dve.tensor_tensor(logit[:], logit[:], gb[:], ALU.add))
            step(dve.tensor_reduce(mx[:], logit[:], X, ALU.max))
            step(dve.tensor_scalar(prob[:], logit[:], mx[:], None, ALU.subtract))
            assert n[0] == PRE_EXP
            step(dve.tensor_tensor(wins[:], over_f(logit), over_e(logit), ALU.is_gt))
            step(dve.tensor_tensor(ties[:], over_f(logit), over_e(logit), ALU.is_equal))
            step(dve.tensor_tensor(ties[:], ties[:], before[:], ALU.mult))
            step(dve.tensor_tensor(wins[:], wins[:], ties[:], ALU.add))
            step(dve.tensor_reduce(rank[:], wins[:], X, ALU.add))
            step(dve.tensor_tensor(chosen[:], over_k(rank), slot_no[:], ALU.is_equal))
            step(dve.tensor_tensor(number[:], chosen[:], number[:], ALU.mult))
            step(dve.tensor_reduce(idx_f[:], number[:], X, ALU.add))
            step(dve.tensor_copy(idx_i[:], idx_f[:]))
            dve.wait_ge(exped, 1)
            step(dve.tensor_reduce(total[:], prob[:], X, ALU.add))
            step(dve.reciprocal(total[:], total[:]))
            step(dve.tensor_scalar(prob[:], prob[:], total[:], None, ALU.mult))
            step(dve.tensor_tensor(chosen[:], chosen[:], over_k(prob), ALU.mult))
            step(dve.tensor_reduce(wts[:], chosen[:], X, ALU.add))
            assert n[0] == ALL


HG = 4
GROUPS = H // HG
PT = H // 2
KQ = 3 * HD
SHIFT_ROW = KQ
KC = S // P
STEPS = GROUPS * KC * 2
LEAD = 11
RING = 4
SLOTS = 28
QK, V_FIRST, PROJ, V_REST, TURN_Y, HID, FF = 0, 4, 6, 10, 12, 16, 24
QK_STEPS = {1: (0,), 3: (1,), 5: (2,), 7: (3,)}
SUMS_STEP, NORM_STEPS = 1, {7: (0,), 8: (1, 2, 3)}
PROJ_STEPS = {9: (0,), 10: (1,), 11: (2,), 12: (3,)}
V_STEPS = {8: (0, 1), 13: (2, 3)}
TURN_Y_STEPS = {14: (0, 1, 2, 3)}
HID_STEPS = {15 + m: (m,) for m in range(M)}
FF_STEPS = {23 + n: (n,) for n in range(2 * T)}
AT_TURN = 5


def raw_place(g, odd):
    return GROUPS if odd and g == 0 else g


def v_slot(t):
    return V_FIRST + t if t < 2 else V_REST + t - 2


def slot_count(i, n):
    before = 4 + 4 + (i - 1) * (SLOTS // 2)
    if isinstance(i, int) and i <= 0:
        before, n = (0 if i < 0 else 4), n if n < PROJ else n - 4
    elif isinstance(i, int) and i >= PAIRS - 1:
        before, n = before - (4 if i == PAIRS else 0), n - 6 if n < TURN_Y else n - 8
    return before + (n // 2 + 1)


def stage_b(nc, dram, x2_dram, x2T_dram, qk_dram, z_dram, out, keep):
    with ExitStack() as ctx:
        def sb(name, shape, dt=F32):
            return ctx.enter_context(nc.sbuf_tensor(name, shape, dt))

        def ps(name, shape):
            return ctx.enter_context(nc.psum_tensor(name, shape, F32))

        def sem(name):
            return ctx.enter_context(nc.semaphore("b_" + name))

        st_banks, max_banks = ps("b_st", [P, 2, 512]), ps("b_max", [P, 2, 512])
        o_bank, turn_bank = ps("b_o", [P, 512]), ps("b_turn", [P, 512])
        shared = [ps("b_shared0", [P, 512]), ps("b_shared1", [P, 512])]

        ident, index, weight = keep["ident"], keep["index"], keep["weight"]
        w_qkv = sb("w_qkv", [P, C, 3 * D])
        w_out = sb("w_out", [P, GROUPS, D])
        w_1 = sb("w_1", [P, C, F])
        w_2 = sb("w_2", [P, M, D])
        b_qk, b_hid = sb("b_qk", [P, 4]), sb("b_hid", [P, M])
        b_v = sb("b_v", [P, D])
        rows = sb("rows", [P, 5, D])
        x2T = sb("x2T_b", [P, C, S])
        x2 = sb("x2_b", [P, T, D])
        acc = sb("acc", [P, T, D])
        qk32 = sb("qk32", [P, 4, S])
        qk_parts = sb("qk_parts", [P, 4, 2, S], F32R)
        q_stack = sb("q_stack", [P, PT, S], F32R)
        k_stack = sb("k_stack", [P, PT, S], F32R)
        v_aug = sb("v_aug", [P, TOPK, KC, H, 2 * HD])
        neg_max = sb("neg_max", [P, GROUPS, T, HG])
        shift = sb("shift", [HG, S], F32R)
        prob = sb("prob_b", [P, RING, 2, S])
        o_raw = sb("o_raw", [P, GROUPS + 1, S])
        z_turned = sb("z_turned", [P, H * S // P])
        rz_turned = sb("rz_turned", [P, H * S // P])
        rz = sb("rz_b", [P, GROUPS, S])
        o_norm = sb("o_norm", [P, GROUPS, S])
        r = sb("r", [P, 2, D])
        y1 = sb("y1", [P, T, D])
        y1_b = sb("y1_b", [P, T, D])
        y1T = sb("y1T", [P, C, S])
        hidden = sb("hidden_b", [P, M, S])
        stats, mv, rstd = sb("stats_b", [P, 6]), sb("mv_b", [P, 2]), sb("rstd_b", [P, 1])
        var_eps, minus_half = sb("var_eps_b", [P, 1]), sb("minus_half_b", [P, 1])
        spare, spare_pool = sb("spare_b", [P, 1]), sb("spare_pool", [P, 4])
        w_pair = sb("w_pair", [P, 1])

        consts_set = sem("consts_set")
        x2T_in, rows_in = sem("x2T_in"), sem("rows_in")
        qkv_in, w_out_in, w_1_in, w_2_in = sem("qkv_in"), sem("w_out_in"), sem("w_1_in"), sem("w_2_in")
        x2_in, acc_in = sem("x2_in"), sem("acc_in")
        slot_mm = [sem("slot_mm0"), sem("slot_mm1")]
        slot_taken = [sem("slot_taken0"), sem("slot_taken1")]
        qk_high, qk_low = sem("qk_high"), sem("qk_low")
        qk_out = [sem(f"qk_out{u}") for u in range(4)]
        stacks_in = [sem("stacks_in_a"), sem("stacks_in_b")]
        max_mm, max_done = sem("max_mm"), sem("max_done")
        turn_mm, shift_sb, shift_in = sem("turn_mm"), sem("shift_sb"), sem("shift_in")
        st_mm, prob_ready, pv_mm, o_sb = sem("st_mm"), sem("prob_ready"), sem("pv_mm"), sem("o_sb")
        z_moved, z_inverted, rz_moved, rz_in, o_ready = (sem("z_moved"), sem("z_inverted"), sem("rz_moved"),
                                                         sem("rz_in"), sem("o_ready"))
        y1_ready, y1b_ready = sem("y1_ready"), sem("y1b_ready")
        acc_ready, stored = sem("acc_ready"), sem("stored")
        half_set, var_ready, rstd_ready = sem("half_set"), sem("var_ready"), sem("rstd_ready")
        dve_step = sem("dve_step")

        block = ctx.enter_context(nc.Block())

        def in_order(pair_iteration):
            def run(eng):
                pair_iteration(0, 0, PAIRS)
                pair_iteration(1, 1, PAIRS - 1)
                with eng.Fori(1, B - 1) as batch:
                    pair_iteration(batch * TOPK, 2, 4)
                    pair_iteration(batch * TOPK + 1, 3, 3)
                pair_iteration(PAIRS - 2, 2, 2)
                pair_iteration(PAIRS - 1, 3, 1)
            return run

        @block.sync
        def _(sp):
            def expert_of(i):
                return sp.value_load(index[:, bass.ds(i, 1)], min_val=0, max_val=E - 1)

            def whole(src, e):
                return src[bass.ds(e, 1)]

            def load_qkv(n, e, even):
                sp.dma_start(w_qkv[:], whole(dram["w_qkv"], e).rearrange("o p c n -> p (o c) n")).then_inc(qkv_in, DMA)
                sp.dma_start(b_qk[:], whole(dram["b_qk"], e).rearrange("o p n -> p (o n)")).then_inc(qkv_in, DMA)
                sp.dma_start(b_v[:], whole(dram["b_v"], e).to_broadcast([P, D])).then_inc(qkv_in, DMA)
                if even:
                    sp.dma_start(x2T[:], x2T_dram[bass.ds(n // TOPK, 1)].rearrange("o p c n -> p (o c) n")).then_inc(x2T_in, DMA)

            def load_w_out(e):
                for j in range(HG):
                    sp.dma_start(w_out[32 * j:32 * j + HD, :, :],
                                 whole(dram["w_out"], e)[:, j].rearrange("o p g n -> p (o g) n")).then_inc(w_out_in, DMA)
                sp.dma_start(w_out[HD:HD + 1, 0, :], whole(dram["b_out"], e)).then_inc(w_out_in, DMA)

            def load_w_1(e):
                sp.dma_start(w_1[:], whole(dram["w_1"], e).rearrange("o p c n -> p (o c) n")).then_inc(w_1_in, DMA)
                sp.dma_start(b_hid[:], whole(dram["b_hid"], e).rearrange("o p n -> p (o n)")).then_inc(w_1_in, DMA)

            def load_rows(e):
                sp.dma_start(rows[:], whole(dram["rows"], e).to_broadcast([P, 5, D])).then_inc(rows_in, DMA)

            def load_w_2(e):
                sp.dma_start(w_2[:], whole(dram["w_2"], e).rearrange("o p m n -> p (o m) n")).then_inc(w_2_in, DMA)

            def load_x2(n):
                sp.dma_start(x2[:], x2_dram[bass.ds(n // TOPK, 1)].rearrange("o (t p) d -> p (o t) d", p=P)).then_inc(x2_in, DMA)

            def load_sums(n):
                sp.dma_start(acc[:], out[bass.ds(n // TOPK, 1)].rearrange("o (t p) d -> p (o t) d", p=P)).then_inc(acc_in, DMA)

            def parts_out(n):
                for u in range(4):
                    sp.wait_ge(qk_high, n * 4 + (u + 1))
                    sp.wait_ge(qk_low, n * 4 + (u + 1))
                    sp.dma_start(qk_dram[u], qk_parts[:, u, :, :].bitcast(F32)).then_inc(qk_out[u], DMA)

            def stacks_back(n, half):
                for u in range(4):
                    sp.wait_ge(qk_out[u], n * DMA + DMA)
                    odd = u % 2
                    stack, order = (q_stack, (0, 0, 1)) if u < 2 else (k_stack, (0, 1, 0))
                    for block_no, part in enumerate(order):
                        row = 64 * odd + HD * block_no
                        sp.dma_start(stack[row:row + HD, 4 * half:4 * half + 4, :].bitcast(F32),
                                     qk_dram[u, 64 * half:64 * half + 64, part, :].rearrange(
                                         "(m p) n -> p m n", p=HD)).then_inc(stacks_in[half], DMA)

            def shift_rows(n, g):
                sp.wait_ge(shift_sb, n * GROUPS + (g + 1))
                for j in range(HG):
                    row = 64 * (j % 2) + SHIFT_ROW
                    sp.dma_start(q_stack[row:row + 1, 2 * g + j // 2, :].bitcast(F32),
                                 shift[j:j + 1, :].bitcast(F32)).then_inc(shift_in, DMA)

            def store_sums(n):
                sp.dma_start(out[bass.ds(n // TOPK, 1)].rearrange("o (t p) d -> p (o t) d", p=P), acc[:]).then_inc(stored, DMA)

            first, second = expert_of(0), expert_of(1)
            sp.wait_ge(consts_set, 3)
            load_qkv(0, first, True)
            parts_out(0)
            stacks_back(0, 0)
            stacks_back(0, 1)
            for n in (0, 1):
                sp.wait_ge(slot_taken[n], slot_count(-1, v_slot(2 + n)))
            load_qkv(1, second, False)
            shift_rows(0, 0)

            def iteration(i, before, left):
                even = before % 2 == 0
                e_here = expert_of(i)
                if before:
                    e_last = expert_of(i - 1)
                if left > 2:
                    e_ahead = expert_of(i + 2)
                if before:
                    sp.wait_ge(st_mm, i * STEPS)
                    stacks_back(i, 1)
                    if before >= 2:
                        sp.wait_ge(acc_ready, (i - 1) * T)
                    sp.wait_ge(z_moved, i * (2 * DMA))
                    load_rows(e_last)
                shift_rows(i, 1)
                if before:
                    load_w_2(e_last)
                if left > 1:
                    parts_out(i + 1)
                if before:
                    load_w_1(e_last)
                if before and not even:
                    if before >= 3:
                        store_sums(i - 2)
                        sp.wait_ge(stored, (i - 1) // TOPK * DMA)
                    load_sums(i - 1)
                shift_rows(i, 2)
                if before:
                    for n in (0, 1):
                        sp.wait_ge(slot_taken[n], slot_count(i, PROJ + 2 + n))
                load_w_out(e_here)
                if even:
                    load_x2(i)
                if left > 2:
                    for n in (0, 1):
                        sp.wait_ge(slot_taken[n], slot_count(i, v_slot(2 + n)))
                    load_qkv(i + 2, e_ahead, even)
                if left > 1:
                    sp.wait_ge(st_mm, i * STEPS + STEPS // 2)
                    stacks_back(i + 1, 0)
                shift_rows(i, 3)
                if left > 1:
                    shift_rows(i + 1, 0)

            in_order(iteration)(sp)
            e_last = expert_of(PAIRS - 1)
            sp.wait_ge(acc_ready, (PAIRS - 1) * T)
            load_rows(e_last)
            load_w_2(e_last)
            load_w_1(e_last)
            for t in range(T):
                sp.wait_ge(acc_ready, (PAIRS - 1) * T + (t + 1))
                sp.dma_start(out[B - 1, t * P:(t + 1) * P, :], acc[:, t, :]).then_inc(stored, DMA)
            sp.wait_ge(stored, (B - 1 + T) * DMA)

        @block.tensor
        def _(pe):
            def slot(i, n):
                if due(slot_count(i, n) - 1):
                    pe.wait_ge(slot_taken[n % 2], slot_count(i, n) - 1)
                return shared[n % 2]

            def stack_rows(h, extra):
                first = 64 * (h % 2)
                return slice(first, first + KQ + extra)

            def qk_tile(i, u, c, even):
                if u == 0 and c == 0:
                    pe.wait_ge(qkv_in, i * (3 * DMA) + 6 * DMA)
                    if even:
                        pe.wait_ge(x2T_in, (i + 1) // TOPK * DMA + DMA)
                bank = slot(i, QK + u) if c == 0 else shared[u % 2]
                product = pe.matmul(bank[:], w_qkv[:, c, u * P:(u + 1) * P], x2T[:, c, :], start=(c == 0), stop=(c == C - 1))
                if c == C - 1:
                    product.then_inc(slot_mm[u % 2], 1)

            def v_tile(i, t):
                bank = slot(i, v_slot(t))
                for c in range(C):
                    last = pe.matmul(bank[:, 0:D], x2T[:, c, t * P:(t + 1) * P], w_qkv[:, c, 2 * D:3 * D],
                                     start=(c == 0), stop=(c == C - 1))
                last.then_inc(slot_mm[t % 2], 1)

            def maxima(i, s):
                n, m = (i, s) if s < STEPS else (i + 1, s - STEPS)
                g, qc, j = m // 8, m % 8 // 2, 2 * (m % 2)
                if m % (STEPS // 2) == 0:
                    pe.wait_ge(stacks_in[m // (STEPS // 2)], n * (12 * DMA) + 12 * DMA)
                if due(n * STEPS + m):
                    pe.wait_ge(max_done, n * STEPS + m)
                for k in range(2):
                    h = HG * g + j + k
                    last = pe.matmul(max_banks[:, k, :], q_stack[stack_rows(h, 0), h // 2, qc * P:(qc + 1) * P],
                                     k_stack[stack_rows(h, 0), h // 2, :], start=True, stop=True)
                last.then_inc(max_mm, 1)

            def turn_maxima(n, g):
                pe.wait_ge(max_done, n * STEPS + 8 * (g + 1))
                if due(n * GROUPS + g):
                    pe.wait_ge(shift_sb, n * GROUPS + g)
                for qc in range(T):
                    last = pe.transpose(turn_bank[0:HG, qc * P:(qc + 1) * P], neg_max[:, g, qc, :], ident[:])
                last.then_inc(turn_mm, 1)

            def scores(i, s):
                g, kc, half = s // 8, s % 8 // 2, s % 2
                if s % 8 == 0:
                    pe.wait_ge(shift_in, i * (H * DMA) + (g + 1) * (HG * DMA))
                if due(i * STEPS + s):
                    pe.wait_ge(prob_ready, i * STEPS + s)
                for k in range(2):
                    h = HG * g + 2 * half + k
                    last = pe.matmul(st_banks[:, k, :], k_stack[stack_rows(h, 1), h // 2, kc * P:(kc + 1) * P],
                                     q_stack[stack_rows(h, 1), h // 2, :], start=True, stop=True)
                last.then_inc(st_mm, 1)

            def times_v(i, s, odd):
                g, kc = s // 8, s % 8 // 2
                pe.wait_ge(prob_ready, i * STEPS + (s + 1))
                if kc == 0:
                    if due(i * GROUPS + g):
                        pe.wait_ge(o_sb, i * GROUPS + g)
                if s == 1:
                    for n in (0, 1):
                        pe.wait_ge(slot_taken[n], slot_count(i - 1, v_slot(2 + n)))
                for j in range(HG):
                    last = pe.matmul(o_bank[32 * j:32 * j + 32, :], v_aug[:, odd, kc, HG * g + j, :],
                                     prob[:, (s - 1 + j // 2) % RING, j % 2, :], start=(kc == 0), stop=(kc == KC - 1))
                last.then_inc(pv_mm, 1)

            def project(i, t):
                if t == 0:
                    pe.wait_ge(w_out_in, i * (5 * DMA))
                    pe.wait_ge(o_ready, i * GROUPS)
                bank = slot(i, PROJ + t)
                for g in range(GROUPS):
                    last = pe.matmul(bank[:, 0:D], o_norm[:, g, t * P:(t + 1) * P], w_out[:, g, :],
                                     start=(g == 0), stop=(g == GROUPS - 1))
                last.then_inc(slot_mm[t % 2], 1)

            def turn_y(i, t):
                pe.wait_ge(y1_ready, (i - 1) * T + (t + 1))
                bank = slot(i, TURN_Y + t)
                for c in range(C):
                    last = pe.transpose(bank[:, c * P:(c + 1) * P], y1[:, t, c * P:(c + 1) * P], ident[:])
                last.then_inc(slot_mm[t % 2], 1)

            def hidden_chunk(i, m):
                if m == 0:
                    pe.wait_ge(w_1_in, i * (2 * DMA))
                    for n in (0, 1):
                        pe.wait_ge(slot_taken[n], slot_count(i, TURN_Y + 2 + n))
                bank = slot(i, HID + m)
                for c in range(C):
                    last = pe.matmul(bank[:], w_1[:, c, m * P:(m + 1) * P], y1T[:, c, :], start=(c == 0), stop=(c == C - 1))
                last.then_inc(slot_mm[m % 2], 1)

            def feed_forward(i, t, half):
                if t == 0 and half == 0:
                    pe.wait_ge(w_2_in, i * DMA)
                    for n in (0, 1):
                        pe.wait_ge(slot_taken[n], slot_count(i, HID + 6 + n))
                bank = slot(i, FF + t) if half == 0 else shared[t % 2]
                for m in range(4 * half, 4 * half + 4):
                    last = pe.matmul(bank[:, 0:D], hidden[:, m, t * P:(t + 1) * P], w_2[:, m, :],
                                     start=(m == 0), stop=(m == M - 1))
                if half == 1:
                    last.then_inc(slot_mm[t % 2], 1)

            def of_last_pair(i, s):
                for t in PROJ_STEPS.get(s, ()):
                    project(i, t)
                for t in TURN_Y_STEPS.get(s, ()):
                    turn_y(i, t)
                for m in HID_STEPS.get(s, ()):
                    hidden_chunk(i, m)
                for n in FF_STEPS.get(s, ()):
                    feed_forward(i, n // 2, n % 2)

            pe.wait_ge(consts_set, 3)
            for u in range(4):
                for c in range(C):
                    qk_tile(-1, u, c, True)
            for t in range(T):
                v_tile(-1, t)
            for s in range(LEAD):
                maxima(0, s)
            turn_maxima(0, 0)

            def iteration(i, before, left):
                for s in range(STEPS):
                    scores(i, s)
                    if left > 1:
                        for u in QK_STEPS.get(s + 1, ()):
                            qk_tile(i, u, 0, before % 2 == 1)
                        for u in QK_STEPS.get(s, ()):
                            qk_tile(i, u, 1, before % 2 == 1)
                        for t in V_STEPS.get(s, ()):
                            v_tile(i, t)
                    if before:
                        of_last_pair(i, s)
                    if s % 8 == AT_TURN:
                        if s // 8 + 1 < GROUPS:
                            turn_maxima(i, s // 8 + 1)
                        elif left > 1:
                            turn_maxima(i + 1, 0)
                    if left > 1 or LEAD + s < STEPS:
                        maxima(i, LEAD + s)
                    if s % 2 == 1:
                        times_v(i, s, before % 2)

            in_order(iteration)(pe)
            for s in range(STEPS):
                of_last_pair(PAIRS, s)

        @block.scalar
        def _(act):
            def slot(i, n):
                act.wait_ge(slot_mm[n % 2], slot_count(i, n))
                return shared[n % 2]

            def high_part(n, u):
                act.wait_ge(slot_taken[u % 2], slot_count(n - 1, QK + u))
                act.copy(qk_parts[:, u, 0, :], qk32[:, u, :]).then_inc(qk_high, 1)

            def take_shift(n, g):
                act.wait_ge(turn_mm, n * GROUPS + (g + 1))
                if due(n * (H * DMA) + g * (HG * DMA)):
                    act.wait_ge(shift_in, n * (H * DMA) + g * (HG * DMA))
                act.copy(shift[:], turn_bank[0:HG, :]).then_inc(shift_sb, 1)

            def of_last_pair(i, s):
                for t in TURN_Y_STEPS.get(s, ()):
                    bank = slot(i, TURN_Y + t)
                    act.copy(y1T[:, :, t * P:(t + 1) * P],
                             bank[:, 0:D].rearrange("p (c n) -> p c n", c=C)).then_inc(slot_taken[t % 2], 1)
                for m in HID_STEPS.get(s, ()):
                    if m == 0:
                        act.wait_ge(w_1_in, i * (2 * DMA))
                    bank = slot(i, HID + m)
                    act.activation(hidden[:, m, :], bank[:], ACT.Relu, bias=b_hid[:, m:m + 1]).then_inc(slot_taken[m % 2], 1)

            for u in range(4):
                high_part(0, u)
            take_shift(0, 0)

            def iteration(i, before, left):
                for s in range(STEPS):
                    act.wait_ge(st_mm, i * STEPS + (s + 1))
                    if due(i * (STEPS // 2) + (s - RING) // 2 + 1):
                        act.wait_ge(pv_mm, i * (STEPS // 2) + (s - RING) // 2 + 1)
                    act.activation(prob[:, s % RING, :, :].rearrange("p n q -> p (n q)"),
                                   st_banks[:].rearrange("p n q -> p (n q)"), ACT.Exp).then_inc(prob_ready, 1)
                    if left > 1:
                        for u in QK_STEPS.get(s - 1, ()):
                            high_part(i + 1, u)
                    if before:
                        of_last_pair(i, s)
                    if s % 8 == AT_TURN:
                        if s // 8 + 1 < GROUPS:
                            take_shift(i, s // 8 + 1)
                        elif left > 1:
                            take_shift(i + 1, 0)
                    if s % 8 == 7:
                        g = s // 8
                        act.wait_ge(pv_mm, i * (STEPS // 2) + (s + 1) // 2)
                        if g == 1:
                            if due(i * GROUPS):
                                act.wait_ge(o_ready, i * GROUPS)
                        act.copy(o_raw[:, raw_place(g, before % 2), :], o_bank[:]).then_inc(o_sb, 1)

            in_order(iteration)(act)
            for s in range(STEPS):
                of_last_pair(PAIRS, s)

        @block.gpsimd
        def _(pool):
            pool.memset(minus_half[:], -0.5).then_inc(half_set, 1)
            pool.wait_ge(half_set, 1)
            pool.memset(spare_pool[:], 0.0)

            def low_part(n, u):
                if u == 0:
                    for half in range(2):
                        if due(n * (12 * DMA)):
                            pool.wait_ge(stacks_in[half], n * (12 * DMA))
                pool.wait_ge(qk_high, n * 4 + (u + 1))
                pool.tensor_tensor(qk_parts[:, u, 1, :], qk32[:, u, :], qk_parts[:, u, 0, :].bitcast(F32),
                                   ALU.subtract).then_inc(qk_low, 1)

            def inverse_root(n, k):
                pool.wait_ge(var_ready, n * (2 * T) + (k + 1))
                pool.tensor_tensor(rstd[:], var_eps[:], minus_half[:], ALU.pow).then_inc(rstd_ready, 1)

            def wait_then_dma(k, sem, value):
                pool.wait_ge(sem, value)
                pool.tensor_tensor(spare_pool[:, k:k + 1], minus_half[:], minus_half[:], ALU.add)

            def spread_sums(n, k, odd):
                if k == 0:
                    wait_then_dma(k, o_sb, n * GROUPS + GROUPS)
                    pool.dma_start(z_dram[0], o_raw[HD:P:2 * HD, odd:odd + GROUPS, :]).then_inc(z_moved, DMA)
                if k == 1:
                    wait_then_dma(k, z_moved, n * (2 * DMA) + DMA)
                    pool.dma_start(z_turned[:], z_dram[0].rearrange("j g (a n) -> (j g a) n", n=H * S // P)).then_inc(z_moved, DMA)
                if k == 2:
                    wait_then_dma(k, z_inverted, n + 1)
                    pool.dma_start(z_dram[1].rearrange("j g (a n) -> (j g a) n", n=H * S // P), rz_turned[:]).then_inc(rz_moved, DMA)
                if k == 3:
                    wait_then_dma(k, rz_moved, n * DMA + DMA)
                    for j in range(HG):
                        pool.dma_start(rz[32 * j:32 * j + 32, :, :],
                                       z_dram[1, j].unsqueeze(0).to_broadcast([32, GROUPS, S])).then_inc(rz_in, DMA)

            def norms(n):
                inverse_root(n, 0)
                for t in range(T):
                    if t + 1 < T:
                        inverse_root(n, t + 1)
                    pool.wait_ge(y1_ready, n * T + (t + 1))
                    pool.tensor_tensor(y1_b[:, t, :], y1[:, t, :], rows[:, 0, :], ALU.add).then_inc(y1b_ready, 1)
                for t in range(T):
                    inverse_root(n, T + t)

            for u in range(4):
                low_part(0, u)

            def iteration(i, before, left):
                if before:
                    spread_sums(i - 1, 0, (before - 1) % 2)
                    spread_sums(i - 1, 1, (before - 1) % 2)
                    spread_sums(i - 1, 2, (before - 1) % 2)
                if left > 1:
                    low_part(i + 1, 0)
                if before:
                    spread_sums(i - 1, 3, (before - 1) % 2)
                if left > 1:
                    low_part(i + 1, 1)
                    low_part(i + 1, 2)
                    low_part(i + 1, 3)
                if before:
                    norms(i - 1)

            in_order(iteration)(pool)
            for k in range(4):
                spread_sums(PAIRS - 1, k, 1)
            norms(PAIRS - 1)

        @block.vector
        def _(dve):
            dve.memset(w_out[:], 0.0).then_inc(consts_set, 1)
            dve.memset(k_stack[:].bitcast(F32), 1.0).then_inc(consts_set, 1)
            dve.memset(v_aug[:], 1.0).then_inc(consts_set, 1)
            dve.wait_ge(consts_set, 3)
            OWN = T * 3 + T * 4 + 1
            own = [0]

            def step(n, ins):
                own[0] += 1
                ins.then_inc(dve_step, 1)
                dve.wait_ge(dve_step, n * OWN + own[0])

            def slot(i, n):
                dve.wait_ge(slot_mm[n % 2], slot_count(i, n))
                return shared[n % 2]

            def full_qk(i, u):
                if u == 0:
                    dve.wait_ge(qkv_in, i * (3 * DMA) + 6 * DMA)
                if due((i + 1) * 4 + (u - 3)):
                    dve.wait_ge(qk_low, (i + 1) * 4 + (u - 3))
                bank = slot(i, QK + u)
                dve.tensor_scalar(qk32[:, u, :], bank[:], b_qk[:, u:u + 1], float(HD) ** -0.5 if u < 2 else 1.0,
                                  ALU.add, ALU.mult).then_inc(slot_taken[u % 2], 1)

            def take_v(i, t, odd):
                if t == 0:
                    if due(i * (STEPS // 2)):
                        dve.wait_ge(pv_mm, i * (STEPS // 2))
                bank = slot(i, v_slot(t))
                dve.tensor_tensor(v_aug[:, odd, t, :, 0:HD], bank[:, 0:D].rearrange("p (h d) -> p h d", h=H),
                                  b_v[:].rearrange("p (h d) -> p h d", h=H), ALU.add).then_inc(slot_taken[t % 2], 1)

            def reduce_max(i, s):
                n, m = (i, s) if s < STEPS else (i + 1, s - STEPS)
                g, qc, j = m // 8, m % 8 // 2, 2 * (m % 2)
                dve.wait_ge(max_mm, n * STEPS + (m + 1))
                dve.tensor_reduce(neg_max[:, g, qc, j:j + 2], max_banks[:], X, ALU.max, negate=True).then_inc(max_done, 1)

            def norm_begin(n, k, rt, w):
                step(n, dve.bn_stats(stats[:], rt))
                dve.memset(spare[:], 0.0)
                step(n, dve.bn_aggr(mv[:], stats[:]))
                dve.tensor_scalar(var_eps[:], mv[:, 1:2], EPS, None, ALU.add).then_inc(var_ready, 1)
                step(n, dve.scalar_tensor_tensor(out=rt, in0=rt, scalar=mv[:, 0:1], in1=rows[:, w, :],
                                                 op0=ALU.subtract, op1=ALU.mult))

            def norm_end(n, k, dst, rt, b):
                dve.wait_ge(rstd_ready, n * (2 * T) + (k + 1))
                return dve.scalar_tensor_tensor(out=dst, in0=rt, scalar=rstd[:], in1=rows[:, b, :],
                                                op0=ALU.mult, op1=ALU.add)

            def first_begin(i, t, odd):
                n, rt = i - 1, r[:, t % 2, :]
                if t == 0:
                    dve.wait_ge(rows_in, i * DMA)
                    if odd:
                        dve.wait_ge(x2_in, (i + 1) // TOPK * DMA)
                bank = slot(i, PROJ + t)
                dve.tensor_tensor(rt, bank[:, 0:D], x2[:, t, :], ALU.add).then_inc(slot_taken[t % 2], 1)
                dve.wait_ge(slot_taken[t % 2], slot_count(i, PROJ + t))
                norm_begin(n, t, rt, 1)

            def first_end(i, t):
                n, rt = i - 1, r[:, t % 2, :]
                norm_end(n, t, y1[:, t, :], rt, 2).then_inc(y1_ready, 1)

            def second_begin(i, t):
                n, rt = i - 1, r[:, t % 2, :]
                dve.wait_ge(y1b_ready, n * T + (t + 1))
                bank = slot(i, FF + t)
                dve.tensor_tensor(rt, bank[:, 0:D], y1_b[:, t, :], ALU.add).then_inc(slot_taken[t % 2], 1)
                dve.wait_ge(slot_taken[t % 2], slot_count(i, FF + t))
                norm_begin(n, T + t, rt, 3)

            def second_end(i, t, odd):
                n, rt = i - 1, r[:, t % 2, :]
                step(n, norm_end(n, T + t, rt, rt, 4))
                if t == 0 and odd:
                    dve.wait_ge(acc_in, (i + 1) // TOPK * DMA)
                dve.scalar_tensor_tensor(out=acc[:, t, :], in0=rt, scalar=w_pair[:], in1=acc[:, t, :],
                                         op0=ALU.mult, op1=ALU.add).then_inc(acc_ready, 1)

            def divide(i, s, odd):
                for g in NORM_STEPS.get(s, ()):
                    if g == 0:
                        dve.wait_ge(rz_in, i * (HG * DMA))
                    place = raw_place(g, odd)
                    dve.tensor_tensor(o_norm[:, g, :], o_raw[:, place, :], rz[:, place - odd, :], ALU.mult).then_inc(o_ready, 1)

            def of_last_pair(i, s, before):
                if s == SUMS_STEP:
                    own[0] = 0
                    if before >= 2:
                        dve.wait_ge(acc_ready, (i - 1) * T)
                    step(i - 1, dve.tensor_copy(w_pair[:], weight[:, bass.ds(i - 1, 1)]))
                    dve.wait_ge(z_moved, i * (2 * DMA))
                    dve.reciprocal(rz_turned[:], z_turned[:]).then_inc(z_inverted, 1)
                for t in PROJ_STEPS.get(s - 1, ()):
                    first_end(i, t)
                for t in PROJ_STEPS.get(s, ()):
                    first_begin(i, t, before % 2)
                for n in FF_STEPS.get(s, ()):
                    if n % 2 == 1:
                        second_begin(i, n // 2)
                for n in FF_STEPS.get(s - 1, ()):
                    if n % 2 == 1:
                        second_end(i, n // 2, before % 2)

            for u in range(4):
                full_qk(-1, u)
            for t in range(T):
                take_v(-1, t, 0)
            for s in range(LEAD):
                reduce_max(0, s)

            def iteration(i, before, left):
                for s in range(STEPS):
                    for t in V_STEPS.get(s, ()):
                        if left > 1:
                            take_v(i, t, (before + 1) % 2)
                    if before:
                        divide(i, s, (before - 1) % 2)
                    if left > 1 or LEAD + s < STEPS:
                        reduce_max(i, LEAD + s)
                    for u in QK_STEPS.get(s, ()):
                        if left > 1:
                            full_qk(i, u)
                    if before:
                        of_last_pair(i, s, before)
                assert own[0] in (0, OWN)

            in_order(iteration)(dve)
            for s in range(STEPS):
                divide(PAIRS, s, 1)
                of_last_pair(PAIRS, s, PAIRS)


def build(nc, dram, out):
    x2_dram = nc.dram_tensor("x2_scratch", (B, S, D), F32, kind="Internal").ap()
    x2T_dram = nc.dram_tensor("x2T_scratch", (B, P, C, S), F32, kind="Internal").ap()
    qk_dram = nc.dram_tensor("qk_scratch", (4, P, 2, S), F32, kind="Internal").ap()
    z_dram = nc.dram_tensor("z_scratch", (2, HG, GROUPS, S), F32, kind="Internal").ap()
    index_dram = nc.dram_tensor("index_scratch", (PAIRS,), I32, kind="Internal").ap()
    weight_dram = nc.dram_tensor("weight_scratch", (PAIRS,), F32, kind="Internal").ap()
    with ExitStack() as ctx:
        keep = {name: ctx.enter_context(nc.sbuf_tensor(name, shape, dt)) for name, shape, dt in (
            ("ident", [P, P], F32), ("colsum", [P, C, B], F32), ("index", [1, PAIRS], I32), ("weight", [P, PAIRS], F32))}
        stage_a(nc, dram, x2_dram, x2T_dram, out, keep)
        gate(nc, dram, index_dram, weight_dram, keep)
        stage_b(nc, dram, x2_dram, x2T_dram, qk_dram, z_dram, out, keep)


def kernel(**inputs):
    import numpy as np
    import concourse.bacc as bacc
    from concourse.bass_utils import run_bass_kernel_spmd

    def arr(name):
        return np.asarray(inputs[name])

    iw, ib = arr("L0_ffn_in_proj_w"), arr("L0_ffn_in_proj_b")

    def even_odd(a):
        return a.reshape(E, PT, 2, HD, -1).transpose(0, 2, 1, 3, 4).reshape(E, D, -1)

    qkv = np.concatenate([even_odd(iw[:, 0:D]), even_odd(iw[:, D:2 * D]), iw[:, 2 * D:]], axis=1)
    b_qk = np.concatenate([even_odd(ib[:, 0:D]), even_odd(ib[:, D:2 * D])], axis=1).reshape(E, 4, P)
    e = np.arange(E)
    arrays = {
        "x": arr("x"),
        "ctxT": arr("ctx_1024").reshape(B * SC, D).T,
        "Wk": arr("L0_xattn_W_k"), "Wv": arr("L0_xattn_W_v"),
        "WqT": arr("L0_xattn_W_q").reshape(D, H, DK).transpose(2, 1, 0),
        "Wo": arr("L0_xattn_W_o").reshape(H, DK, D).transpose(1, 0, 2),
        "gate_wT": arr("L0_ffn_gate_w").T,
        "gate_b": np.broadcast_to(arr("L0_ffn_gate_b"), (B, E)),
        "w_qkv": qkv.reshape(E, 3 * D, C, P).transpose(0, 3, 2, 1),
        "b_qk": b_qk.transpose(0, 2, 1),
        "b_hid": arr("L0_ffn_lin1_b").reshape(E, M, P).transpose(0, 2, 1),
        "b_v": ib[:, 2 * D:],
        "w_out": arr("L0_ffn_out_proj_w").reshape(E, D, GROUPS, HG, HD).transpose(0, 3, 4, 2, 1),
        "b_out": arr("L0_ffn_out_proj_b"),
        "w_1": arr("L0_ffn_lin1_w").reshape(E, F, C, P).transpose(0, 3, 2, 1),
        "w_2": arr("L0_ffn_lin2_w").reshape(E, D, M, P).transpose(0, 3, 2, 1),
        "rows": np.stack([arr("L0_ffn_" + n) for n in ("lin2_b", "ln1_w", "ln1_b", "ln2_w", "ln2_b")], axis=1),
        "ident": np.eye(P, dtype=np.float32),
        "before": np.broadcast_to(e[None, :] < e[:, None], (B, E, E)).astype(np.float32),
        "number": np.broadcast_to(e, (B, TOPK, E)).astype(np.float32),
        "slot_no": np.broadcast_to(np.arange(TOPK)[:, None], (B, TOPK, E)).astype(np.float32),
    }
    nc = bacc.Bacc("TRN2", target_bir_lowering=False, num_devices=1)
    arrays = {f"in_{n}": np.ascontiguousarray(a) for n, a in arrays.items()}
    dram = {n[3:]: nc.dram_tensor(n, a.shape, mybir.dt.from_np(a.dtype), kind="ExternalInput").ap()
            for n, a in arrays.items()}
    out = nc.dram_tensor("out", (B, S, D), F32, kind="ExternalOutput").ap()
    build(nc, dram, out)
    r = run_bass_kernel_spmd(nc, [arrays], core_ids=[0])
    return r.results[0]["out"]
```
